# Optimizing a Trainium2 kernel written in Bass

```python
import numpy as np
import jax
import jax.numpy as jnp

def _softmax(x, axis=-1):
    return jax.nn.softmax(x, axis=axis)

def _gelu(x):
    return jax.nn.gelu(x, approximate=True)

def _silu(x):
    return jax.nn.silu(x)

def _sigmoid(x):
    return jax.nn.sigmoid(x)

def _layernorm(x, axis=-1, eps=1e-05):
    m = jnp.mean(x, axis=axis, keepdims=True)
    v = jnp.var(x, axis=axis, keepdims=True)
    return (x - m) / jnp.sqrt(v + eps)

def _scatter_add(tgt, idx, src, axis=0):
    return tgt.at[idx].add(src)

def _segment_sum(src, seg, n):
    return jax.ops.segment_sum(src, seg, n)
kernel_name = 'mk_prb_d2_jaxref_r4_63808b'

def setup_inputs(seed: int=0):
    np.random.seed(seed)
    _w = jnp.asarray

    def _L0_attn_setup():
        import jax, jax.numpy as jnp
        import numpy as np
        LN_EPS = 1e-05
        key = jax.random.key(seed)
        k_u, k_B, k_C = jax.random.split(key, 3)
        Bsz, L, d_model, d_state = (8, 1024, 256, 64)
        u = jax.random.normal(k_u, (Bsz, L, d_model), dtype=jnp.float32)
        log_neg_real = -0.5 * jnp.ones((d_state,), jnp.float32)
        imag = jnp.arange(1, d_state + 1, dtype=jnp.float32)
        B_mat = jax.random.normal(k_B, (d_state, d_model), jnp.float32) / d_model ** 0.5
        C_mat = jax.random.normal(k_C, (d_model, d_state), jnp.float32) / d_state ** 0.5
        D = jnp.zeros((d_model,), jnp.float32)
        gamma = jnp.ones((d_model,), jnp.float32)
        beta = jnp.zeros((d_model,), jnp.float32)
        return {'u': u, 'log_neg_real': log_neg_real, 'imag': imag, 'B_mat': B_mat, 'C_mat': C_mat, 'D': D, 'gamma': gamma, 'beta': beta}
    _L0_attn_in = _L0_attn_setup()

    def _L0_ffn_setup():
        import jax, jax.numpy as jnp
        import numpy as np
        from jax import lax
        HIDDEN = 256
        INTER = 128
        E = 64
        K = 6
        G = 8
        TG = 4
        NSH = 2
        ISH = INTER * NSH

        def _moe_forward(hidden_states, gate_w, gate_bias, eg_w, eu_w, ed_w, sg_w, su_w, sd_w):
            B, S, H = hidden_states.shape
            x = hidden_states.reshape(-1, H)
            T = x.shape[0]
            shared = jax.nn.silu(x @ sg_w.T) * (x @ su_w.T) @ sd_w.T
            logits = x @ gate_w.T
            scores = jax.nn.sigmoid(logits) + gate_bias
            group_scores = scores.reshape(T, G, E // G).max(axis=-1)
            _, sel_groups = lax.top_k(group_scores, TG)
            group_mask = jnp.zeros((T, G), scores.dtype).at[jnp.arange(T)[:, None], sel_groups].set(1.0)
            mask = jnp.repeat(group_mask, E // G, axis=1)
            masked_scores = scores * mask
            topk_w, topk_i = lax.top_k(masked_scores, K)
            topk_w = topk_w / (topk_w.sum(axis=-1, keepdims=True) + 1e-08)
            comb = jnp.zeros((T, E), x.dtype).at[jnp.arange(T)[:, None], topk_i].add(topk_w)
            h = jax.nn.silu(jnp.einsum('th,eih->eti', x, eg_w)) * jnp.einsum('th,eih->eti', x, eu_w)
            routed = jnp.einsum('eti,ehi,te->th', h, ed_w, comb)
            return (shared + routed).reshape(B, S, H)
        key = jax.random.key(seed)
        ks = jax.random.split(key, 9)
        s = 0.02
        return {'hidden_states': jax.random.normal(ks[0], (1, 256, HIDDEN), jnp.float32), 'gate_w': jax.random.normal(ks[1], (E, HIDDEN), jnp.float32) * s, 'gate_bias': jnp.zeros((E,), jnp.float32), 'eg_w': jax.random.normal(ks[2], (E, INTER, HIDDEN), jnp.float32) * s, 'eu_w': jax.random.normal(ks[3], (E, INTER, HIDDEN), jnp.float32) * s, 'ed_w': jax.random.normal(ks[4], (E, HIDDEN, INTER), jnp.float32) * s, 'sg_w': jax.random.normal(ks[5], (ISH, HIDDEN), jnp.float32) * s, 'su_w': jax.random.normal(ks[6], (ISH, HIDDEN), jnp.float32) * s, 'sd_w': jax.random.normal(ks[7], (HIDDEN, ISH), jnp.float32) * s}
    _L0_ffn_in = _L0_ffn_setup()

    def _L1_attn_setup():
        import jax, jax.numpy as jnp
        import numpy as np
        B, S, D = (4, 512, 256)
        H, C = (16, 64)
        HID = H * C
        key = jax.random.key(seed)
        ks = jax.random.split(key, 9)
        scale = 0.02
        return {'x': jax.random.normal(ks[0], (B, S, D), dtype=jnp.float32), 'Wq': jax.random.normal(ks[1], (D, HID), dtype=jnp.float32) * scale, 'bq': jnp.zeros((HID,), dtype=jnp.float32), 'Wk': jax.random.normal(ks[2], (D, HID), dtype=jnp.float32) * scale, 'bk': jnp.zeros((HID,), dtype=jnp.float32), 'Wv': jax.random.normal(ks[3], (D, HID), dtype=jnp.float32) * scale, 'bv': jnp.zeros((HID,), dtype=jnp.float32), 'Wo': jax.random.normal(ks[4], (HID, D), dtype=jnp.float32) * scale, 'bo': jnp.zeros((D,), dtype=jnp.float32)}
    _L1_attn_in = _L1_attn_setup()

    def _L1_ffn_setup():
        import jax, jax.numpy as jnp
        import numpy as np
        DIM = 256
        HIDDEN = 768
        SCALE = 1.0 / 127.0

        def _dequant(w_int, dtype):
            return w_int.astype(dtype) * jnp.asarray(SCALE, dtype)
        key = jax.random.key(seed)
        k_x, k_g, k_u, k_d = jax.random.split(key, 4)
        x = jax.random.normal(k_x, (4, 512, DIM), dtype=jnp.float32)
        w_gate = jax.random.randint(k_g, (HIDDEN, DIM), -127, 128, dtype=jnp.int32)
        w_up = jax.random.randint(k_u, (HIDDEN, DIM), -127, 128, dtype=jnp.int32)
        w_down = jax.random.randint(k_d, (DIM, HIDDEN), -127, 128, dtype=jnp.int32)
        return {'x': x, 'w_gate': w_gate, 'w_up': w_up, 'w_down': w_down}
    _L1_ffn_in = _L1_ffn_setup()
    _d = {'L0_attn_u': _L0_attn_in['u'], 'L0_attn_log_neg_real': _L0_attn_in['log_neg_real'], 'L0_attn_imag': _L0_attn_in['imag'], 'L0_attn_B_mat': _L0_attn_in['B_mat'], 'L0_attn_C_mat': _L0_attn_in['C_mat'], 'L0_attn_D': _L0_attn_in['D'], 'L0_attn_gamma': _L0_attn_in['gamma'], 'L0_attn_beta': _L0_attn_in['beta'], 'L0_ffn_gate_w': _L0_ffn_in['gate_w'], 'L0_ffn_gate_bias': _L0_ffn_in['gate_bias'], 'L0_ffn_eg_w': _L0_ffn_in['eg_w'], 'L0_ffn_eu_w': _L0_ffn_in['eu_w'], 'L0_ffn_ed_w': _L0_ffn_in['ed_w'], 'L0_ffn_sg_w': _L0_ffn_in['sg_w'], 'L0_ffn_su_w': _L0_ffn_in['su_w'], 'L0_ffn_sd_w': _L0_ffn_in['sd_w'], 'L1_attn_Wq': _L1_attn_in['Wq'], 'L1_attn_bq': _L1_attn_in['bq'], 'L1_attn_Wk': _L1_attn_in['Wk'], 'L1_attn_bk': _L1_attn_in['bk'], 'L1_attn_Wv': _L1_attn_in['Wv'], 'L1_attn_bv': _L1_attn_in['bv'], 'L1_attn_Wo': _L1_attn_in['Wo'], 'L1_attn_bo': _L1_attn_in['bo'], 'L1_ffn_w_gate': _L1_ffn_in['w_gate'], 'L1_ffn_w_up': _L1_ffn_in['w_up'], 'L1_ffn_w_down': _L1_ffn_in['w_down']}
    _x0 = _d['L0_attn_u']
    _d['L0_attn_u'] = jax.random.normal(jax.random.fold_in(jax.random.key(seed), 1), (4, 1024, 256), dtype=_x0.dtype)
    del _x0
    return _d

def reference(L0_attn_u, L0_attn_log_neg_real, L0_attn_imag, L0_attn_B_mat, L0_attn_C_mat, L0_attn_D, L0_attn_gamma, L0_attn_beta, L0_ffn_gate_w, L0_ffn_gate_bias, L0_ffn_eg_w, L0_ffn_eu_w, L0_ffn_ed_w, L0_ffn_sg_w, L0_ffn_su_w, L0_ffn_sd_w, L1_attn_Wq, L1_attn_bq, L1_attn_Wk, L1_attn_bk, L1_attn_Wv, L1_attn_bv, L1_attn_Wo, L1_attn_bo, L1_ffn_w_gate, L1_ffn_w_up, L1_ffn_w_down):

    def _L0_attn_ref(u, log_neg_real, imag, B_mat, C_mat, D, gamma, beta):
        import jax, jax.numpy as jnp
        import numpy as np
        LN_EPS = 1e-05
        Bsz, L, d_model = u.shape
        d_state = log_neg_real.shape[0]
        a = jax.lax.complex(-jnp.exp(log_neg_real), imag)
        a_bar = jnp.exp(a)
        b_bar = ((a_bar - 1.0) / a)[:, None] * B_mat.astype(a.dtype)
        Bu = jnp.einsum('bld,nd->bln', u.astype(a.dtype), b_bar)

        def step(h, x_t):
            h = h * a_bar + x_t
            return (h, h)
        h0 = jnp.zeros((Bsz, d_state), a.dtype)
        _, hs = jax.lax.scan(step, h0, jnp.swapaxes(Bu, 0, 1))
        hs = jnp.swapaxes(hs, 0, 1)
        y = jnp.einsum('bln,dn->bld', hs, C_mat.astype(a.dtype)).real + D * u
        x = u + y
        mu = jnp.mean(x, axis=-1, keepdims=True)
        var = jnp.mean((x - mu) ** 2, axis=-1, keepdims=True)
        return (x - mu) * jax.lax.rsqrt(var + LN_EPS) * gamma + beta

    def _L0_ffn_ref(hidden_states, gate_w, gate_bias, eg_w, eu_w, ed_w, sg_w, su_w, sd_w):
        import jax, jax.numpy as jnp
        import numpy as np
        from jax import lax
        HIDDEN = 256
        INTER = 128
        E = 64
        K = 6
        G = 8
        TG = 4
        NSH = 2
        ISH = INTER * NSH

        def _moe_forward(hidden_states, gate_w, gate_bias, eg_w, eu_w, ed_w, sg_w, su_w, sd_w):
            B, S, H = hidden_states.shape
            x = hidden_states.reshape(-1, H)
            T = x.shape[0]
            shared = jax.nn.silu(x @ sg_w.T) * (x @ su_w.T) @ sd_w.T
            logits = x @ gate_w.T
            scores = jax.nn.sigmoid(logits) + gate_bias
            group_scores = scores.reshape(T, G, E // G).max(axis=-1)
            _, sel_groups = lax.top_k(group_scores, TG)
            group_mask = jnp.zeros((T, G), scores.dtype).at[jnp.arange(T)[:, None], sel_groups].set(1.0)
            mask = jnp.repeat(group_mask, E // G, axis=1)
            masked_scores = scores * mask
            topk_w, topk_i = lax.top_k(masked_scores, K)
            topk_w = topk_w / (topk_w.sum(axis=-1, keepdims=True) + 1e-08)
            comb = jnp.zeros((T, E), x.dtype).at[jnp.arange(T)[:, None], topk_i].add(topk_w)
            h = jax.nn.silu(jnp.einsum('th,eih->eti', x, eg_w)) * jnp.einsum('th,eih->eti', x, eu_w)
            routed = jnp.einsum('eti,ehi,te->th', h, ed_w, comb)
            return (shared + routed).reshape(B, S, H)
        return _moe_forward(hidden_states, gate_w, gate_bias, eg_w, eu_w, ed_w, sg_w, su_w, sd_w)

    def _L1_attn_ref(x, Wq, bq, Wk, bk, Wv, bv, Wo, bo):
        import jax, jax.numpy as jnp
        import numpy as np
        B, S, D = (4, 512, 256)
        H, C = (16, 64)
        HID = H * C
        b, s, _ = x.shape
        inv_sqrt_c = jnp.asarray(1.0 / C ** 0.5, dtype=x.dtype)
        Q = (x @ Wq + bq).reshape(b, s, H, C) * inv_sqrt_c
        K = (x @ Wk + bk).reshape(b, s, H, C)
        V = (x @ Wv + bv).reshape(b, s, H, C)
        scores = jnp.einsum('bshq,bshk->bshqk', Q, K)
        mask = jnp.triu(jnp.ones((C, C), dtype=bool), 1)
        scores = jnp.where(mask, jnp.asarray(-jnp.inf, scores.dtype), scores)
        w = jax.nn.softmax(scores, axis=-1)
        attn = jnp.einsum('bshqk,bshk->bshq', w, V)
        attn = attn.reshape(b, s, HID)
        return attn @ Wo + bo

    def _L1_ffn_ref(x, w_gate, w_up, w_down):
        import jax, jax.numpy as jnp
        import numpy as np
        DIM = 256
        HIDDEN = 768
        SCALE = 1.0 / 127.0

        def _dequant(w_int, dtype):
            return w_int.astype(dtype) * jnp.asarray(SCALE, dtype)
        wg = _dequant(w_gate, x.dtype)
        wu = _dequant(w_up, x.dtype)
        wd = _dequant(w_down, x.dtype)
        gate = jnp.einsum('bsd,hd->bsh', x, wg)
        up = jnp.einsum('bsd,hd->bsh', x, wu)
        h = jax.nn.silu(gate) * up
        return jnp.einsum('bsh,dh->bsd', h, wd)
    x = L0_attn_u
    xn = _layernorm(x, axis=-1)
    x = x + _L0_attn_ref(xn, L0_attn_log_neg_real, L0_attn_imag, L0_attn_B_mat, L0_attn_C_mat, L0_attn_D, L0_attn_gamma, L0_attn_beta) + _L0_ffn_ref(xn, L0_ffn_gate_w, L0_ffn_gate_bias, L0_ffn_eg_w, L0_ffn_eu_w, L0_ffn_ed_w, L0_ffn_sg_w, L0_ffn_su_w, L0_ffn_sd_w)
    xn = _layernorm(x, axis=-1)
    x = x + _L1_attn_ref(xn, L1_attn_Wq, L1_attn_bq, L1_attn_Wk, L1_attn_bk, L1_attn_Wv, L1_attn_bv, L1_attn_Wo, L1_attn_bo) + _L1_ffn_ref(xn, L1_ffn_w_gate, L1_ffn_w_up, L1_ffn_w_down)
    return x

_drawn_inputs = setup_inputs


def setup_inputs(seed=0):
    import zlib

    import numpy as np

    out = dict(_drawn_inputs(seed))
    spreads = {'L0_attn_log_neg_real': (-0.5, 0.6),
     'L0_attn_D': (0.0, 0.1),
     'L0_attn_gamma': (1.0, 0.2),
     'L0_attn_beta': (0.0, 0.269),
     'L0_ffn_gate_bias': (0.0, 0.8),
     'L1_attn_bq': (0.0, 2.0),
     'L1_attn_bk': (0.0, 2.0),
     'L1_attn_bv': (0.0, 2.0),
     'L1_attn_bo': (0.0, 2.0)}
    factors = {'L0_ffn_gate_w': 8.0,
     'L0_ffn_eg_w': 8.0,
     'L0_ffn_eu_w': 8.0,
     'L0_ffn_ed_w': 8.0,
     'L0_ffn_sg_w': 4.821,
     'L0_ffn_su_w': 4.775,
     'L0_ffn_sd_w': 4.776,
     'L1_attn_Wq': 64.0,
     'L1_attn_Wk': 64.0,
     'L1_attn_Wv': 64.0,
     'L1_attn_Wo': 64.0}
    for name, (base, spread) in spreads.items():
        noise = np.random.default_rng([zlib.crc32(name.encode()), seed]).standard_normal(out[name].shape)
        drawn = base * np.exp(spread * noise) if base else spread * noise
        out[name] = jnp.asarray(drawn.astype(out[name].dtype))
    for name, factor in factors.items():
        out[name] = (out[name] * factor).astype(out[name].dtype)
    return out
```

```python
from contextlib import ExitStack

import concourse.bass as bass
from concourse import mybir

ALU = mybir.AluOpType
ACT = mybir.ActivationFunctionType
AX = mybir.AxisListType
F32 = mybir.dt.float32
I32 = mybir.dt.int32

P = 128
BATCH, SEQ, D = 4, 1024, 256
T = BATCH * SEQ
NT = T // P
DC = D // P
NS = 64
E, GROUPS, TOPG, TOPK = 64, 8, 4, 6
EG = E // GROUPS
INTER = 128
NSH = 2
SLOT_BLOCKS = T * TOPK // P + E
SLOTS = SLOT_BLOCKS * P
H, C = 16, 64
HC = H * C
HID = 768
HT = HID // P
QS = C + 2
EPS = 1e-5
LOG_SEQ = 10
TWO_PI_HI, TWO_PI_MID, TWO_PI_LO = 6.28125, 0.0019350051879882812, 3.019916050561733e-07
ROUND_MAGIC = 12582912.0
INV_TWO_PI = 0.15915494309189535


def view(ap, dims, offset=0):
    return bass.AP(tensor=ap.tensor, offset=ap.offset + offset, ap=[list(ap.ap[0])] + [list(d) for d in dims])


def wait(eng, sem, value):
    if isinstance(value, int) and value <= 0:
        return
    eng.wait_ge(sem, value)


def settle(eng, sem):
    eng.sem_inc(sem, 1)


class Chain:

    def __init__(self, eng, sem):
        self.eng, self.sem, self.n = eng, sem, 0

    def __call__(self, ins):
        self.mark(ins)
        self.join()

    def mark(self, ins):
        self.n += 1
        ins.then_inc(self.sem, 1)

    def join(self):
        self.eng.wait_ge(self.sem, self.n)


class Alloc:
    def __init__(self, nc, ctx, tag):
        self.nc, self.ctx, self.tag = nc, ctx, tag

    def sb(self, name, shape, dt=F32):
        return self.ctx.enter_context(self.nc.sbuf_tensor(f"{self.tag}_{name}", shape, dt))

    def ps(self, name, shape=(P, 512), dt=F32):
        return self.ctx.enter_context(self.nc.psum_tensor(f"{self.tag}_{name}", list(shape), dt))

    def sem(self, name):
        return self.ctx.enter_context(self.nc.semaphore(f"{self.tag}_{name}"))


def tokens(ap):
    return ap.rearrange("(n p) d -> p n d", p=P)


def make_constants(nc, a, k):
    k.ident = a.sb("ident", [P, P])
    k.upper = a.sb("upper", [P, P])
    k.ones = a.sb("ones", [P, P])
    k.tri8 = a.sb("tri8", [P, GROUPS, GROUPS])
    k.top_half = a.sb("top_half", [P, 1])
    k.iota_p = a.sb("iota_p", [P, 2])
    k.tokid = a.sb("tokid", [P, NT])
    k.minus_half = a.sb("minus_half", [P, NT])
    s = a.sem("const")
    with nc.Block() as block:

        @block.gpsimd
        def _(pool):
            c = Chain(pool, s)
            c.mark(nc.gpsimd.memset(k.ident[:], 0.0))
            c.mark(nc.gpsimd.memset(k.upper[:], 1.0))
            c.mark(nc.gpsimd.memset(k.ones[:], 1.0))
            c.mark(nc.gpsimd.memset(k.tri8[:], 1.0))
            c.mark(nc.gpsimd.memset(k.top_half[:], 1.0))
            c.mark(nc.gpsimd.memset(k.minus_half[:], -0.5))
            c.join()
            c.mark(nc.gpsimd.affine_select(out=k.ident[:], in_=k.ident[:], compare_op=ALU.not_equal, fill=1.0,
                                           base=0, pattern=[[-1, P]], channel_multiplier=1))
            c.mark(nc.gpsimd.affine_select(out=k.upper[:], in_=k.upper[:], compare_op=ALU.is_gt, fill=0.0,
                                           base=0, pattern=[[1, P]], channel_multiplier=-1))
            c.mark(nc.gpsimd.affine_select(out=k.tri8[:], in_=k.tri8[:], compare_op=ALU.is_gt, fill=0.0,
                                           base=0, pattern=[[1, GROUPS], [-1, GROUPS]], channel_multiplier=0))
            c.mark(nc.gpsimd.affine_select(out=k.top_half[:], in_=k.top_half[:], compare_op=ALU.is_gt, fill=0.0,
                                           base=NS, pattern=[[0, 1]], channel_multiplier=-1))
            c.mark(nc.gpsimd.iota(k.iota_p[:], [[P, 2]], base=0, channel_multiplier=1,
                                  allow_small_or_imprecise_dtypes=True))
            c.mark(nc.gpsimd.iota(k.tokid[:], [[P, NT]], base=0, channel_multiplier=1,
                                  allow_small_or_imprecise_dtypes=True))
            c.join()


def normalise_and_score(nc, k, io, scratch):
    with ExitStack() as ctx:
        a = Alloc(nc, ctx, "ln")
        gate_wT = a.sb("gate_wT", [P, DC, E])
        stats = a.sb("stats", [P, NT, 6])
        mv = a.sb("mv", [P, NT, 2])
        rstd = a.sb("rstd", [P, NT])
        tr = [a.ps(f"tr{i}", [P, DC, P]) for i in range(2)]
        logits = a.ps("logits", [P, NT, E])
        w_in, moments, pow_done, xn_done = (a.sem(s) for s in ("w_in", "moments", "pow", "xn"))
        x_in = [a.sem(f"x_in{q}") for q in range(4)]
        turned, evacuated, logit_done, score_done, xn_out = (
            a.sem(s) for s in ("turned", "evac", "logit", "score", "xn_out"))
        dve_step, pool_step = a.sem("dve"), a.sem("pool")
        PER = NT // 4
        with nc.Block() as block:

            @block.sync
            def _(sp):
                for q in range(4):
                    sp.dma_start(k.x[:, q * PER:(q + 1) * PER, :],
                                 tokens(io["u"])[:, q * PER:(q + 1) * PER, :]).then_inc(x_in[q], 16)
                sp.dma_start(gate_wT[:], io["gate_wT"].rearrange("(c p) e -> p c e", p=P)).then_inc(w_in, 16)
                sp.dma_start(k.gate_bias[:], io["gate_bias"].partition_broadcast(P)).then_inc(w_in, 16)
                for q in range(4):
                    sp.wait_ge(xn_done, (q + 1) * PER)
                    sp.dma_start(tokens(scratch["xn"])[:, q * PER:(q + 1) * PER, :],
                                 k.xn[:, q * PER:(q + 1) * PER, :]).then_inc(xn_out, 16)
                sp.wait_ge(xn_out, 64)

            @block.vector
            def _(dve):
                c = Chain(dve, dve_step)
                for n in range(NT):
                    if n % PER == 0:
                        dve.wait_ge(x_in[n // PER], 16)
                    c.mark(nc.vector.bn_stats(stats[:, n, :], k.x[:, n, :]))
                c.join()
                for n in range(NT):
                    nc.vector.bn_aggr(mv[:, n, :], stats[:, n, :]).then_inc(moments, 1)
                dve.wait_ge(pow_done, 1)
                for n in range(NT):
                    nc.vector.tensor_scalar(k.xn[:, n, :], k.x[:, n, :], mv[:, n, 0:1], rstd[:, n:n + 1],
                                            ALU.subtract, ALU.mult).then_inc(xn_done, 1)

            @block.gpsimd
            def _(pool):
                c = Chain(pool, pool_step)
                pool.wait_ge(moments, NT)
                c(nc.gpsimd.tensor_scalar(rstd[:], mv[:, :, 1], EPS, None, ALU.add))
                nc.gpsimd.tensor_tensor(rstd[:], rstd[:], k.minus_half[:], ALU.pow).then_inc(pow_done, 1)

            @block.tensor
            def _(pe):
                def score(n):
                    pe.wait_ge(evacuated, n + 1)
                    for c in range(DC):
                        ins = nc.tensor.matmul(logits[:, n, :], k.xnT[:, c, n * P:(n + 1) * P], gate_wT[:, c, :],
                                               start=(c == 0), stop=(c == DC - 1), skip_group_check=True)
                    ins.then_inc(logit_done, 1)

                pe.wait_ge(w_in, 32)
                for n in range(NT):
                    pe.wait_ge(xn_done, n + 1)
                    wait(pe, evacuated, n - 1)
                    for c in range(DC):
                        ins = nc.tensor.transpose(tr[n % 2][:, c, :], k.xn[:, n, c * P:(c + 1) * P], k.ident[:])
                    ins.then_inc(turned, 1)
                    if n:
                        score(n - 1)
                score(NT - 1)

            @block.scalar
            def _(act):
                for n in range(NT):
                    act.wait_ge(turned, n + 1)
                    nc.scalar.copy(k.xnT[:, :, n * P:(n + 1) * P], tr[n % 2][:]).then_inc(evacuated, 1)
                for q in range(4):
                    act.wait_ge(logit_done, NT)
                    nc.scalar.activation(k.score[:, q * 8:(q + 1) * 8, :], logits[:, q * 8:(q + 1) * 8, :],
                                         ACT.Sigmoid).then_inc(score_done, 1)
                act.wait_ge(score_done, 4)


def route(nc, k, io, scratch):
    with ExitStack() as ctx:
        a = Alloc(nc, ctx, "rt")
        gm = a.sb("gm", [P, NT, GROUPS])
        rank = a.sb("rank", [P, NT, GROUPS])
        cmpa = a.sb("cmpa", [P, NT * E])
        cmpb = a.sb("cmpb", [P, NT * E])
        keep = a.sb("keep", [P, NT * E])
        sel = a.sb("sel", [P, NT, E])
        comb = a.sb("comb", [P, NT, E])
        key = a.sb("key", [P, NT, E])
        tot = a.sb("tot", [P, E, NT])
        excl = a.sb("excl", [P, E, NT])
        keep_t = a.sb("keep_t", [P, E, NT])
        top8 = a.sb("top8", [P, NT, 8])
        small = a.sb("small", [P, NT])
        blocks_i = a.sb("blocks_i", [P, E], I32)
        blocks = a.sb("blocks", [P, E])
        ends = a.sb("ends", [P, E])
        base = a.sb("base", [P, E])
        cmpe = a.sb("cmpe", [P, 2, E])
        bexp = a.sb("bexp", [P, 2])
        diag = a.sb("diag", [P, 2, P])
        zeros = a.sb("zeros", [P, SLOTS // P])
        tab = a.sb("tab", [P, 2, P])
        cum = a.ps("cum", [P, NT, E])
        all_ = a.ps("all", [P, NT, E])
        masks, sel_done, cum_done, slots_done, zeroed = (a.sem(s) for s in ("masks", "sel", "cum", "slots", "zeroed"))
        scattered, copied, tab_in, diag_done, bexp_done, widx_done = (
            a.sem(s) for s in ("scattered", "copied", "tab_in", "diag", "bexp", "widx"))
        turned, dve_step = a.sem("turned"), a.sem("dve")

        with nc.Block() as block:

            @block.gpsimd
            def _(pool):
                nc.gpsimd.memset(keep[:], 1.0).then_inc(masks, 1)
                nc.gpsimd.memset(keep_t[:], 1.0).then_inc(masks, 1)
                nc.gpsimd.memset(zeros[:], 0.0).then_inc(masks, 1)
                pool.wait_ge(masks, 3)
                nc.gpsimd.memset(view(keep[:], [[E, NT]]), 0.0).then_inc(masks, 1)
                nc.gpsimd.memset(keep_t[:, :, 0], 0.0).then_inc(masks, 1)
                pool.wait_ge(zeroed, 16)
                pool.wait_ge(slots_done, 1)
                for n in range(NT):
                    for j in range(TOPK):
                        nc.gpsimd.indirect_dma_start(
                            scratch["slot_token"], bass.IndirectOffsetOnAxis(ap=k.slot[:, n, j:j + 1], axis=0),
                            k.tokid[:, n:n + 1], None).then_inc(scattered, 16)
                pool.wait_ge(scattered, 16 * NT * TOPK)

            @block.sync
            def _(sp):
                sp.wait_ge(masks, 3)
                sp.dma_start(scratch["slot_token"].rearrange("(p s) o -> p (s o)", p=P), zeros[:]).then_inc(zeroed, 16)
                sp.wait_ge(zeroed, 16)
                sp.wait_ge(scattered, 16 * NT * TOPK)
                sp.dma_start(tab[:], scratch["slot_token"].rearrange("(c b s) o -> b c (s o)", c=2, s=P)
                             ).then_inc(tab_in, 16)

            @block.vector
            def _(dve):
                c = Chain(dve, dve_step)
                v = nc.vector
                sc = k.score
                c(v.tensor_tensor(sc[:], sc[:], view(k.gate_bias[:], [[0, NT], [1, E]]), ALU.add))
                c(v.tensor_reduce(gm[:], sc[:].rearrange("p n (g e) -> p n g e", g=GROUPS), AX.X, ALU.max))
                other = view(gm[:], [[GROUPS, NT], [0, GROUPS], [1, GROUPS]])
                own = view(gm[:], [[GROUPS, NT], [1, GROUPS], [0, GROUPS]])
                a4 = view(cmpa[:], [[E, NT], [GROUPS, GROUPS], [1, GROUPS]])
                b4 = view(cmpb[:], [[E, NT], [GROUPS, GROUPS], [1, GROUPS]])
                c.mark(v.tensor_tensor(a4, other, own, ALU.is_gt))
                c(v.tensor_tensor(b4, other, own, ALU.is_equal))
                c(v.tensor_tensor(b4, b4, view(k.tri8[:], [[0, NT], [GROUPS, GROUPS], [1, GROUPS]]), ALU.mult))
                c(v.tensor_tensor(cmpa[:], cmpa[:], cmpb[:], ALU.add))
                c(v.tensor_reduce(rank[:], a4, AX.X, ALU.add))
                c(v.tensor_scalar(rank[:], rank[:], float(TOPG), None, ALU.is_lt))
                ms = key
                c(v.tensor_tensor(view(ms[:], [[EG, NT * GROUPS], [1, EG]]), view(sc[:], [[EG, NT * GROUPS], [1, EG]]),
                                  view(rank[:], [[1, NT * GROUPS], [0, EG]]), ALU.mult))
                for n in range(NT):
                    c.mark(v.max(top8[:, n, :], ms[:, n, :]))
                c.join()
                thr = view(top8[:], [[8, NT], [0, E]], TOPK - 1)
                gt = view(cmpa[:], [[E, NT], [1, E]])
                eq = view(cmpb[:], [[E, NT], [1, E]])
                c.mark(v.tensor_tensor(gt, ms[:], thr, ALU.is_gt))
                c(v.tensor_tensor(eq, ms[:], thr, ALU.is_equal))
                c.mark(v.tensor_reduce(small[:], gt, AX.X, ALU.add))
                dve.wait_ge(masks, 5)
                c(v.tensor_tensor_scan(comb[:].rearrange("p n e -> p (n e)"), keep[:], cmpb[:], 0.0, ALU.mult, ALU.add))
                c(v.tensor_scalar(small[:], small[:], -1.0, float(TOPK), ALU.mult, ALU.add))
                c(v.tensor_tensor(comb[:], comb[:], view(small[:], [[1, NT], [0, E]]), ALU.is_le))
                c(v.tensor_tensor(comb[:], comb[:], eq, ALU.mult))
                c(v.tensor_tensor(sel[:], comb[:], gt, ALU.add))
                c(v.tensor_tensor(comb[:], sel[:], ms[:], ALU.mult))
                c(v.tensor_reduce(small[:], comb[:], AX.X, ALU.add))
                c(v.tensor_scalar(small[:], small[:], 1e-8, None, ALU.add))
                c(v.reciprocal(small[:], small[:]))
                v.tensor_tensor(comb[:], comb[:], view(small[:], [[1, NT], [0, E]]), ALU.mult).then_inc(sel_done, 1)
                dve.wait_ge(sel_done, 1)
                dve.wait_ge(cum_done, 2)
                c(v.tensor_copy(tot[:], all_[:].rearrange("p n e -> p e n")))
                c(v.tensor_tensor_scan(excl[:].rearrange("p e n -> p (e n)"), keep_t[:].rearrange("p e n -> p (e n)"),
                                       tot[:].rearrange("p e n -> p (e n)"), 0.0, ALU.mult, ALU.add))
                c(v.tensor_scalar(blocks_i[:], excl[:, :, NT - 1], float(P - 1), None, ALU.add))
                c(v.tensor_scalar(blocks_i[:], blocks_i[:], P.bit_length() - 1, None, ALU.logical_shift_right))
                c(v.tensor_copy(blocks[:], blocks_i[:]))
                c(v.tensor_tensor_scan(ends[:], k.ones[:, 0:E], blocks[:], 0.0, ALU.mult, ALU.add))
                c(v.tensor_tensor(base[:], ends[:], blocks[:], ALU.subtract))
                c(v.tensor_scalar(base[:], base[:], float(P), 1.0, ALU.mult, ALU.add))
                c(v.tensor_tensor(excl[:], excl[:], tot[:], ALU.subtract))
                c(v.tensor_tensor(key[:], cum[:], excl[:].rearrange("p e n -> p n e"), ALU.add))
                c(v.tensor_tensor(key[:], key[:], view(base[:], [[0, NT], [1, E]]), ALU.add))
                c(v.tensor_tensor(key[:], key[:], sel[:], ALU.mult))
                for n in range(NT):
                    c.mark(v.max(top8[:, n, :], key[:, n, :]))
                c.join()
                v.tensor_scalar(k.slot[:], top8[:], -1.0, None, ALU.add).then_inc(slots_done, 1)
                for h in range(2):
                    c.mark(v.tensor_scalar(cmpe[:, h, :], ends[:], k.iota_p[:, h:h + 1], None, ALU.is_le))
                c.join()
                c(v.tensor_reduce(bexp[:], cmpe[:], AX.X, ALU.add))
                c(v.tensor_scalar(bexp[:], bexp[:], float(E - 1), None, ALU.min))
                for h in range(2):
                    v.tensor_scalar(diag[:, h, :], k.ident[:], bexp[:, h:h + 1], None, ALU.mult).then_inc(diag_done, 1)
                dve.wait_ge(bexp_done, 1)
                v.tensor_scalar(k.weight_row[:], all_[:].rearrange("p n e -> p (n e)")[:, 0:2 * P], float(P),
                                k.iota_p[:, 0:1], ALU.mult, ALU.add).then_inc(widx_done, 1)
                for j in range(TOPK):
                    c(v.tensor_tensor(gt, key[:], view(top8[:], [[8, NT], [0, E]], j), ALU.is_equal))
                    c(v.tensor_tensor(gt, gt, comb[:], ALU.mult))
                    c(v.tensor_reduce(k.choice_w[:, j, :], gt, AX.X, ALU.add))
                dve.wait_ge(widx_done, 1)
                dve.wait_ge(turned, 2)
                c(v.tensor_copy(k.slot_tok[:], all_[:].rearrange("p n e -> p (n e)")[:, 512:512 + 2 * P]))

            @block.tensor
            def _(pe):
                pe.wait_ge(sel_done, 1)
                for q in range(4):
                    ins = nc.tensor.matmul(cum[:, q * 8:(q + 1) * 8, :], k.upper[:], sel[:, q * 8:(q + 1) * 8, :],
                                           start=True, stop=True)
                ins.then_inc(cum_done, 1)
                for q in range(4):
                    ins = nc.tensor.matmul(all_[:, q * 8:(q + 1) * 8, :], k.ones[:], sel[:, q * 8:(q + 1) * 8, :],
                                           start=True, stop=True)
                ins.then_inc(cum_done, 1)
                pe.wait_ge(diag_done, 2)
                ins = nc.tensor.matmul(all_[:].rearrange("p n e -> p (n e)")[:, 0:2 * P], k.ones[:],
                                       diag[:].rearrange("p c b -> p (c b)"), start=True, stop=True)
                ins.then_inc(bexp_done, 1)
                pe.wait_ge(tab_in, 16)
                for h in range(2):
                    nc.tensor.transpose(all_[:].rearrange("p n e -> p (n e)")[:, 512 + h * P:512 + (h + 1) * P],
                                        tab[:, h, :], k.ident[:]).then_inc(turned, 1)


def recurrence_and_shared(nc, k, io, scratch):
    with ExitStack() as ctx:
        a = Alloc(nc, ctx, "ssm")
        bT = a.sb("bT", [P, DC, P])
        cT = a.sb("cT", [P, D])
        sgT, suT = a.sb("sgT", [P, DC, NSH * P]), a.sb("suT", [P, DC, NSH * P])
        sdT = a.sb("sdT", [P, NSH, D])
        vec = a.sb("vec", [P, 2])
        d1, gamma, beta = a.sb("d1", [P, D]), a.sb("gamma", [P, D]), a.sb("beta", [P, D])
        sv = a.sb("sv", [P, 24])
        ang, kk, sn, cs = (a.sb(s, [P, LOG_SEQ]) for s in ("ang", "kk", "sn", "cs"))
        ct, st = a.sb("ct", [P, SEQ]), a.sb("st", [P, SEQ])
        wt, rot = a.sb("wt", [P, SEQ]), a.sb("rot", [P, SEQ])
        tmp = a.sb("tmp", [P, SEQ // 2])
        bu, hs = a.sb("bu", [P, 2, SEQ]), a.sb("hs", [P, 2, SEQ])
        xs = a.sb("xs", [P, NT, D])
        stats, mv, rstd = a.sb("stats", [P, NT, 6]), a.sb("mv", [P, NT, 2]), a.sb("rstd", [P, NT])
        sg, sh = a.sb("sg", [P, 2, 512]), a.sb("sh", [P, 2, NSH, 512])
        z = [a.ps(f"z{i}") for i in range(2)]
        y = [a.ps(f"y{i}", [P, D]) for i in range(2)]
        gps, ups = a.ps("gps"), a.ps("ups")
        w_in, moments = a.sem("w_in"), a.sem("moments")
        dve_step, act_step, pool_step = a.sem("dve"), a.sem("act"), a.sem("pool")
        e_done, ang_done, trig_done = a.sem("e"), a.sem("ang"), a.sem("trig")
        z_done, z_free, hs_done, y_done = (a.sem(s) for s in ("z_done", "z_free", "hs_done", "y_done"))
        u_done, skip_done, norm_done, pow_done = (a.sem(s) for s in ("u_done", "skip", "norm", "pow"))
        g_done, silu_done, sh_done, sy_done, sy_free = (
            a.sem(s) for s in ("g_done", "silu", "sh_done", "sy_done", "sy_free"))
        NW = 11
        HALF = SEQ // 512
        with nc.Block() as block:

            @block.sync
            def _(sp):
                for h in range(2):
                    half = slice(h * NS, (h + 1) * NS)
                    sp.dma_start(vec[half, 0:1], io["log_neg_real"]).then_inc(w_in, 16)
                    sp.dma_start(vec[half, 1:2], io["imag"]).then_inc(w_in, 16)
                    sp.dma_start(cT[half, :], io["cT"]).then_inc(w_in, 16)
                    sp.dma_start(bT[:, :, half], io["bT"].rearrange("(c p) n -> p c n", p=P)).then_inc(w_in, 16)
                for dst, name in ((d1, "D"), (gamma, "gamma"), (beta, "beta")):
                    sp.dma_start(dst[:], io[name].partition_broadcast(P)).then_inc(w_in, 16)
                sp.dma_start(sgT[:], io["sgT"].rearrange("(c p) i -> p c i", p=P)).then_inc(w_in, 16)
                sp.dma_start(suT[:], io["suT"].rearrange("(c p) i -> p c i", p=P)).then_inc(w_in, 16)
                sp.dma_start(sdT[:], io["sdT"].rearrange("(c p) h -> p c h", p=P)).then_inc(w_in, 16)

            W_ALL = 16 * 14

            @block.scalar
            def _(act):
                act.wait_ge(w_in, W_ALL)
                c = Chain(act, act_step)
                c(nc.scalar.activation(sv[:, 0:1], vec[:, 0:1], ACT.Exp))
                nc.scalar.activation(sv[:, 1:2], sv[:, 0:1], ACT.Exp, scale=-1.0).then_inc(e_done, 1)
                act.wait_ge(ang_done, 1)
                c.mark(nc.scalar.activation(sn[:], ang[:], ACT.Sin))
                nc.scalar.activation(cs[:], kk[:], ACT.Sin).then_inc(trig_done, 1)
                act.wait_ge(act_step, 2)
                for q in range(T // 512):
                    for i in range(NSH):
                        n = q * NSH + i
                        act.wait_ge(g_done, n + 1)
                        wait(act, sh_done, n - 1)
                        nc.scalar.activation(sg[:, n % 2, :], gps[:], ACT.Silu).then_inc(silu_done, 1)

            @block.gpsimd
            def _(pool):
                pool.wait_ge(w_in, W_ALL)
                c = Chain(pool, pool_step)
                c(nc.gpsimd.tensor_scalar(d1[:], d1[:], 1.0, None, ALU.add))
                for n in range(NT):
                    nc.gpsimd.tensor_tensor(xs[:, n, :], k.xn[:, n, :], d1[:], ALU.mult).then_inc(skip_done, 1)
                for n in range(NT):
                    c.mark(nc.gpsimd.tensor_tensor(k.x[:, n, :], k.x[:, n, :], beta[:], ALU.add))
                c.join()
                pool.wait_ge(moments, NT)
                c(nc.gpsimd.tensor_scalar(rstd[:], mv[:, :, 1], EPS, None, ALU.add))
                nc.gpsimd.tensor_tensor(rstd[:], rstd[:], k.minus_half[:], ALU.pow).then_inc(pow_done, 1)

            @block.vector
            def _(dve):
                v = nc.vector
                c = Chain(dve, dve_step)
                dve.wait_ge(w_in, W_ALL)
                for m in range(LOG_SEQ):
                    c.mark(v.tensor_scalar(ang[:, m:m + 1], vec[:, 1:2], float(2 ** m), None, ALU.mult))
                c.join()
                c(v.tensor_scalar(kk[:], ang[:], INV_TWO_PI, ROUND_MAGIC, ALU.mult, ALU.add))
                c(v.tensor_scalar(kk[:], kk[:], ROUND_MAGIC, None, ALU.subtract))
                for part in (TWO_PI_HI, TWO_PI_MID, TWO_PI_LO):
                    c(v.scalar_tensor_tensor(out=ang[:], in0=kk[:], scalar=-part, in1=ang[:], op0=ALU.mult, op1=ALU.add))
                c(v.tensor_scalar(ang[:], ang[:], 3.1415925, -3.1415925, ALU.min, ALU.max))
                c(v.tensor_scalar(kk[:], ang[:], -1.0, None, ALU.mult))
                c(v.tensor_tensor(kk[:], kk[:], ang[:], ALU.min))
                v.tensor_scalar(kk[:], kk[:], 1.5707963267948966, None, ALU.add).then_inc(ang_done, 1)
                dve.wait_ge(e_done, 1)
                dve.wait_ge(trig_done, 1)
                dve.wait_ge(act_step, 2)
                e, r, w = sv[:, 0:1], sv[:, 1:2], vec[:, 1:2]
                nr, ni, fr, fi, m2, t0 = (sv[:, i:i + 1] for i in range(2, 8))
                al, be, bot = sv[:, 8:9], sv[:, 9:10], sv[:, 10:11]
                c.mark(v.tensor_scalar(nr, cs[:, 0:1], r, -1.0, ALU.mult, ALU.add))
                c.mark(v.tensor_scalar(ni, sn[:, 0:1], r, None, ALU.mult))
                c(v.tensor_tensor(t0, e, e, ALU.mult))
                c(v.scalar_tensor_tensor(out=m2, in0=w, scalar=w, in1=t0, op0=ALU.mult, op1=ALU.add))
                c(v.reciprocal(m2, m2))
                c(v.tensor_tensor(t0, nr, e, ALU.mult))
                c(v.scalar_tensor_tensor(out=fr, in0=ni, scalar=w, in1=t0, op0=ALU.mult, op1=ALU.subtract))
                c(v.tensor_tensor(t0, ni, e, ALU.mult))
                c(v.scalar_tensor_tensor(out=fi, in0=nr, scalar=w, in1=t0, op0=ALU.mult, op1=ALU.add))
                c.mark(v.tensor_scalar(fr, fr, m2, None, ALU.mult))
                c.mark(v.tensor_scalar(bot, k.top_half[:], -1.0, 1.0, ALU.mult, ALU.add))
                c(v.tensor_scalar(fi, fi, m2, -1.0, ALU.mult, ALU.mult))
                c(v.tensor_tensor(t0, fi, bot, ALU.mult))
                c(v.scalar_tensor_tensor(out=al, in0=fr, scalar=k.top_half[:], in1=t0, op0=ALU.mult, op1=ALU.add))
                c(v.tensor_tensor(t0, fr, bot, ALU.mult))
                c(v.scalar_tensor_tensor(out=be, in0=fi, scalar=k.top_half[:], in1=t0, op0=ALU.mult,
                                         op1=ALU.subtract))
                c.mark(v.memset(ct[:, 0:1], 1.0))
                c(v.memset(st[:, 0:1], 0.0))
                for m in range(LOG_SEQ):
                    n = 2 ** m
                    lo, hi = slice(0, n), slice(n, 2 * n)
                    c(v.tensor_scalar(tmp[:, lo], st[:, lo], sn[:, m:m + 1], None, ALU.mult))
                    c(v.scalar_tensor_tensor(out=ct[:, hi], in0=ct[:, lo], scalar=cs[:, m:m + 1], in1=tmp[:, lo],
                                             op0=ALU.mult, op1=ALU.subtract))
                    c(v.tensor_scalar(tmp[:, lo], ct[:, lo], sn[:, m:m + 1], None, ALU.mult))
                    c(v.scalar_tensor_tensor(out=st[:, hi], in0=st[:, lo], scalar=cs[:, m:m + 1], in1=tmp[:, lo],
                                             op0=ALU.mult, op1=ALU.add))
                c.mark(v.tensor_scalar(wt[:], st[:], be, None, ALU.mult))
                c(v.tensor_scalar(rot[:], st[:], bot, -1.0, ALU.mult, ALU.mult))
                c.mark(v.scalar_tensor_tensor(out=wt[:], in0=ct[:], scalar=al, in1=wt[:], op0=ALU.mult, op1=ALU.add))
                c(v.scalar_tensor_tensor(out=rot[:], in0=ct[:], scalar=k.top_half[:], in1=rot[:], op0=ALU.mult,
                                         op1=ALU.add))

                def shared(q):
                    for i in range(NSH):
                        n = q * NSH + i
                        dve.wait_ge(silu_done, n + 1)
                        wait(dve, sy_done, 4 * (q - 1))
                        v.tensor_tensor(sh[:, q % 2, i, :], sg[:, n % 2, :], ups[:], ALU.mult).then_inc(sh_done, 1)

                def add_shared(n):
                    dve.wait_ge(sy_done, n + 1)
                    dve.wait_ge(pool_step, NT + 1)
                    v.tensor_tensor(k.x[:, n, :], k.x[:, n, :], y[n % 2][:], ALU.add).then_inc(sy_free, 1)

                for b in range(BATCH):
                    for h in range(HALF):
                        dve.wait_ge(z_done, b * HALF + h + 1)
                        v.tensor_tensor(bu[:, b % 2, h * 512:(h + 1) * 512], wt[:, h * 512:(h + 1) * 512], z[h][:],
                                        ALU.mult).then_inc(z_free, 1)
                    dve.wait_ge(z_free, (b + 1) * HALF)
                    if b >= 2:
                        dve.wait_ge(y_done, 8 * (b - 1))
                    c(v.tensor_tensor_scan(hs[:, b % 2, :], r.to_broadcast([P, SEQ]), bu[:, b % 2, :], 0.0,
                                           ALU.mult, ALU.add))
                    v.tensor_tensor(hs[:, b % 2, :], hs[:, b % 2, :], rot[:], ALU.mult).then_inc(hs_done, 1)
                    for n in range(8 * b, 8 * b + 8):
                        dve.wait_ge(y_done, n + 1)
                        dve.wait_ge(skip_done, n + 1)
                        v.tensor_tensor(xs[:, n, :], xs[:, n, :], y[n % 2][:], ALU.add).then_inc(u_done, 1)
                        dve.wait_ge(u_done, n + 1)
                        c.mark(v.bn_stats(stats[:, n, :], xs[:, n, :]))
                c.join()
                for n in range(NT):
                    v.bn_aggr(mv[:, n, :], stats[:, n, :]).then_inc(moments, 1)
                for q in range(T // 512):
                    shared(q)
                    if q:
                        for n in range(4 * q - 4, 4 * q):
                            add_shared(n)
                for n in range(NT - 4, NT):
                    add_shared(n)
                dve.wait_ge(sy_free, NT)
                dve.wait_ge(pow_done, 1)
                for n in range(NT):
                    c.mark(v.tensor_scalar(xs[:, n, :], xs[:, n, :], mv[:, n, 0:1], rstd[:, n:n + 1],
                                           ALU.subtract, ALU.mult))
                c.join()
                c(v.tensor_tensor(xs[:], xs[:], view(gamma[:], [[0, NT], [1, D]]), ALU.mult))
                c(v.tensor_tensor(k.x[:], k.x[:], xs[:], ALU.add))

            @block.tensor
            def _(pe):
                pe.wait_ge(w_in, W_ALL)

                def states_in(b):
                    for h in range(HALF):
                        n = b * HALF + h
                        wait(pe, z_free, n - 1)
                        for c in range(DC):
                            ins = nc.tensor.matmul(z[h][:], bT[:, c, :], k.xnT[:, c, n * 512:(n + 1) * 512],
                                                   start=(c == 0), stop=(c == DC - 1))
                        ins.then_inc(z_done, 1)

                states_in(0)
                for b in range(BATCH):
                    if b + 1 < BATCH:
                        states_in(b + 1)
                    pe.wait_ge(hs_done, b + 1)
                    for j in range(8):
                        n = 8 * b + j
                        wait(pe, u_done, n - 1)
                        nc.tensor.matmul(y[n % 2][:], hs[:, b % 2, j * P:(j + 1) * P], cT[:],
                                         start=True, stop=True).then_inc(y_done, 1)

                def up(q):
                    for i in range(NSH):
                        n = q * NSH + i
                        wait(pe, sh_done, n)
                        for dst, w in ((ups, suT), (gps, sgT)):
                            for c in range(DC):
                                ins = nc.tensor.matmul(dst[:], w[:, c, i * P:(i + 1) * P],
                                                       k.xnT[:, c, q * 512:(q + 1) * 512],
                                                       start=(c == 0), stop=(c == DC - 1))
                        ins.then_inc(g_done, 1)

                def down(q):
                    pe.wait_ge(sh_done, NSH * (q + 1))
                    for j in range(4):
                        n = 4 * q + j
                        wait(pe, sy_free, n - 1)
                        for i in range(NSH):
                            ins = nc.tensor.matmul(y[n % 2][:], sh[:, q % 2, i, j * P:(j + 1) * P], sdT[:, i, :],
                                                   start=(i == 0), stop=(i == NSH - 1))
                        ins.then_inc(sy_done, 1)

                pe.wait_ge(u_done, NT)
                up(0)
                for q in range(T // 512):
                    if q + 1 < T // 512:
                        up(q + 1)
                    down(q)


def routed_experts(nc, k, io, scratch):
    RING = 4
    with ExitStack() as ctx:
        a = Alloc(nc, ctx, "moe")
        w = [a.sb(f"w{j}", [P, 3 * D]) for j in range(RING)]
        xr = [a.sb(f"x{j}", [P, D]) for j in range(RING)]
        xT = [a.sb(f"xT{j}", [P, DC, P]) for j in range(RING)]
        gate = [a.sb(f"gate{j}", [P, P]) for j in range(RING)]
        hid = [a.sb(f"hid{j}", [P, P]) for j in range(RING)]
        yo = [a.sb(f"yo{j}", [P, D]) for j in range(RING)]
        wi = [a.sb(f"wi{j}", [P, 1], I32) for j in range(RING)]
        xi = [a.sb(f"xi{j}", [P, 1], I32) for j in range(RING)]
        tr = [a.ps(f"tr{j}", [P, DC, P]) for j in range(2)]
        gu = [a.ps(f"gu{j}", [P, 2, P]) for j in range(2)]
        yp = [a.ps(f"yp{j}", [P, D]) for j in range(2)]
        idx_ready, w_in, x_in, turned, xT_ready, gu_done, gate_ready, hid_ready, y_done, y_ready, y_out = (
            [a.sem(f"{s}{j}") for j in range(RING)]
            for s in ("idx", "w_in", "x_in", "turned", "xT", "gu", "gate", "hid", "y_done", "y_ready", "y_out"))
        weights = io["experts"]
        pool_settled, sp_settled = a.sem("pool_settled"), a.sem("sp_settled")

        def block_loop(eng, blocks):
            blocks(0)
            with eng.Fori(1, SLOT_BLOCKS // RING) as i:
                blocks(i)

        with nc.Block() as block:

            @block.gpsimd
            def _(pool):
                def blocks(i):
                    for j in range(RING):
                        b = i * RING + j
                        wait(pool, w_in[j], i * 16)
                        wait(pool, x_in[j], i * 16)
                        pool.tensor_copy(wi[j][:], k.weight_row[:, bass.ds(b, 1)]).then_inc(idx_ready[j], 1)
                        pool.tensor_copy(xi[j][:], k.slot_tok[:, bass.ds(b, 1)]).then_inc(idx_ready[j], 1)
                        pool.wait_ge(idx_ready[j], i * 2 + 2)
                        wait(pool, turned[j], i)
                        settle(pool, pool_settled)
                        pool.indirect_dma_start(xr[j][:], None, scratch["xn"],
                                                bass.IndirectOffsetOnAxis(ap=xi[j][:], axis=0)).then_inc(x_in[j], 16)
                        wait(pool, y_done[j], i)
                        settle(pool, pool_settled)
                        pool.indirect_dma_start(w[j][:], None, weights,
                                                bass.IndirectOffsetOnAxis(ap=wi[j][:], axis=0)).then_inc(w_in[j], 16)

                block_loop(pool, blocks)

            @block.tensor
            def _(pe):
                def turn(j, i):
                    pe.wait_ge(x_in[j], i * 16 + 16)
                    if j >= 2:
                        pe.wait_ge(xT_ready[j - 2], i + 1)
                    else:
                        wait(pe, xT_ready[j + 2], i)
                    for c in range(DC):
                        ins = nc.tensor.transpose(tr[j % 2][:, c, :], xr[j][:, c * P:(c + 1) * P], k.ident[:])
                    ins.then_inc(turned[j], 1)

                def up(j, i):
                    pe.wait_ge(xT_ready[j], i + 1)
                    pe.wait_ge(w_in[j], i * 16 + 16)
                    if j >= 2:
                        pe.wait_ge(hid_ready[j - 2], i + 1)
                    else:
                        wait(pe, hid_ready[j + 2], i)
                    for s in range(2):
                        for c in range(DC):
                            ins = nc.tensor.matmul(gu[j % 2][:, s, :], w[j][:, (2 * s + c) * P:(2 * s + c + 1) * P],
                                                   xT[j][:, c, :], start=(c == 0), stop=(c == DC - 1))
                    ins.then_inc(gu_done[j], 1)

                def down(j, i):
                    pe.wait_ge(hid_ready[j], i + 1)
                    if j >= 2:
                        pe.wait_ge(y_ready[j - 2], i + 1)
                    else:
                        wait(pe, y_ready[j + 2], i)
                    nc.tensor.matmul(yp[j % 2][:], hid[j][:], w[j][:, 2 * D:3 * D], start=True,
                                     stop=True).then_inc(y_done[j], 1)

                def blocks(i):
                    for j in range(RING + 2):
                        if j < RING:
                            turn(j, i)
                        if 1 <= j <= RING:
                            up(j - 1, i)
                        if j >= 2:
                            down(j - 2, i)

                block_loop(pe, blocks)

            @block.scalar
            def _(act):
                def blocks(i):
                    for j in range(RING + 1):
                        if j < RING:
                            act.wait_ge(gu_done[j], i + 1)
                            wait(act, hid_ready[j], i)
                            nc.scalar.activation(gate[j][:], gu[j % 2][:, 0, :], ACT.Silu).then_inc(gate_ready[j], 1)
                        if j >= 1:
                            act.wait_ge(y_done[j - 1], i + 1)
                            wait(act, y_out[j - 1], i * 16)
                            nc.scalar.copy(yo[j - 1][:], yp[(j - 1) % 2][:]).then_inc(y_ready[j - 1], 1)

                block_loop(act, blocks)

            @block.vector
            def _(dve):
                def blocks(i):
                    for j in range(RING + 1):
                        if j < RING:
                            dve.wait_ge(turned[j], i + 1)
                            wait(dve, gu_done[j], i)
                            nc.vector.tensor_copy(xT[j][:], tr[j % 2][:]).then_inc(xT_ready[j], 1)
                        if j >= 1:
                            dve.wait_ge(gate_ready[j - 1], i + 1)
                            wait(dve, y_done[j - 1], i)
                            nc.vector.tensor_tensor(hid[j - 1][:], gate[j - 1][:], gu[(j - 1) % 2][:, 1, :],
                                                    ALU.mult).then_inc(hid_ready[j - 1], 1)

                block_loop(dve, blocks)

            @block.sync
            def _(sp):
                rows = scratch["slot_out"].rearrange("(b p) d -> p b d", p=P)
                def blocks(i):
                    for j in range(RING):
                        sp.wait_ge(y_ready[j], i + 1)
                        settle(sp, sp_settled)
                        sp.dma_start(rows[:, bass.ds(i * RING + j, 1), :], yo[j][:].unsqueeze(1)).then_inc(y_out[j], 16)
                block_loop(sp, blocks)
                for j in range(RING):
                    sp.wait_ge(y_out[j], 16 * (SLOT_BLOCKS // RING))


def combine(nc, k, io, scratch):
    with ExitStack() as ctx:
        a = Alloc(nc, ctx, "cmb")
        RING = 4
        y = [a.sb(f"y{j}", [P, TOPK, D]) for j in range(RING)]
        bo = a.sb("bo", [P, D])
        stats, mv, rstd = a.sb("stats", [P, NT, 6]), a.sb("mv", [P, NT, 2]), a.sb("rstd", [P, NT])
        xT = a.sb("xT", [P, RING, DC, P])
        tr = [a.ps(f"tr{j}", [P, DC, P]) for j in range(2)]
        summed, moments, pow_done, xn_done, turned, evacuated, x2_done, x2_out, bo_in = (
            a.sem(s) for s in ("summed", "moments", "pow", "xn", "turned", "evac", "x2", "x2_out", "bo_in"))
        y_in, xT_out = ([a.sem(f"{s}{j}") for j in range(RING)] for s in ("y_in", "xT_out"))
        dve_step, pool_step = a.sem("dve"), a.sem("pool")
        with nc.Block() as block:

            @block.gpsimd
            def _(pool):
                for n in range(NT):
                    wait(pool, summed, n - RING + 1)
                    for j in range(TOPK):
                        pool.indirect_dma_start(y[n % RING][:, j, :], None, scratch["slot_out"],
                                                bass.IndirectOffsetOnAxis(ap=k.slot[:, n, j:j + 1], axis=0)
                                                ).then_inc(y_in[n % RING], 16)
                c = Chain(pool, pool_step)
                pool.wait_ge(moments, NT)
                c(nc.gpsimd.tensor_scalar(rstd[:], mv[:, :, 1], EPS, None, ALU.add))
                nc.gpsimd.tensor_tensor(rstd[:], rstd[:], k.minus_half[:], ALU.pow).then_inc(pow_done, 1)

            @block.vector
            def _(dve):
                v = nc.vector
                c = Chain(dve, dve_step)
                for n in range(NT):
                    dve.wait_ge(y_in[n % RING], 16 * TOPK * (n // RING + 1))
                    for j in range(TOPK):
                        ins = v.scalar_tensor_tensor(out=k.x[:, n, :], in0=y[n % RING][:, j, :],
                                                     scalar=k.choice_w[:, j, n:n + 1], in1=k.x[:, n, :],
                                                     op0=ALU.mult, op1=ALU.add)
                        if j < TOPK - 1:
                            c(ins)
                    ins.then_inc(summed, 1)
                    dve.wait_ge(summed, n + 1)
                    c.mark(v.bn_stats(stats[:, n, :], k.x[:, n, :]))
                c.join()
                for n in range(NT):
                    v.bn_aggr(mv[:, n, :], stats[:, n, :]).then_inc(moments, 1)
                dve.wait_ge(pow_done, 1)
                for n in range(NT):
                    v.tensor_scalar(k.xn[:, n, :], k.x[:, n, :], mv[:, n, 0:1], rstd[:, n:n + 1],
                                    ALU.subtract, ALU.mult).then_inc(xn_done, 1)
                dve.wait_ge(xn_done, NT)
                dve.wait_ge(bo_in, 16)
                for q in range(4):
                    v.tensor_tensor(k.x[:, q * 8:(q + 1) * 8, :], k.x[:, q * 8:(q + 1) * 8, :],
                                    view(bo[:], [[0, 8], [1, D]]), ALU.add).then_inc(x2_done, 1)

            @block.tensor
            def _(pe):
                for n in range(NT):
                    pe.wait_ge(xn_done, n + 1)
                    wait(pe, evacuated, n - 1)
                    for c in range(DC):
                        ins = nc.tensor.transpose(tr[n % 2][:, c, :], k.xn[:, n, c * P:(c + 1) * P], k.ident[:])
                    ins.then_inc(turned, 1)

            @block.scalar
            def _(act):
                for n in range(NT):
                    act.wait_ge(turned, n + 1)
                    wait(act, xT_out[n % RING], 16 * (n // RING))
                    nc.scalar.copy(xT[:, n % RING], tr[n % 2][:]).then_inc(evacuated, 1)

            @block.sync
            def _(sp):
                sp.dma_start(bo[:], io["bo"].partition_broadcast(P)).then_inc(bo_in, 16)
                for n in range(NT):
                    sp.wait_ge(evacuated, n + 1)
                    sp.dma_start(scratch["xT"][n], xT[:, n % RING].rearrange("p c t -> p (c t)")
                                 ).then_inc(xT_out[n % RING], 16)
                sp.dma_start(scratch["xT"][NT], xT[:, RING - 1].rearrange("p c t -> p (c t)")
                             ).then_inc(xT_out[RING - 1], 16)
                for q in range(4):
                    sp.wait_ge(x2_done, q + 1)
                    sp.dma_start(tokens(scratch["x2"])[:, q * 8:(q + 1) * 8, :],
                                 k.x[:, q * 8:(q + 1) * 8, :]).then_inc(x2_out, 16)
                sp.wait_ge(x2_out, 64)
                for j in range(RING):
                    sp.wait_ge(xT_out[j], 16 * (NT // RING + (j == RING - 1)))


def plan_chunks():
    cap = H * 2 * (C + 8)
    lengths = list(range(C, 0, -2))
    chunks = []
    while lengths:
        chunk, room = [], cap // (2 * H)
        first = lengths.pop(0)
        chunk.append(first)
        room -= first
        for n in list(lengths):
            if n <= room:
                chunk.append(n)
                lengths.remove(n)
                room -= n
        chunks.append(chunk)
    out = []
    for chunk in chunks:
        off, groups = 0, []
        for n in chunk:
            groups.append((C - n, n, off))
            off += 2 * H * n
        out.append((groups, off))
    return out, cap


CHUNKS, CHUNK_CAP = plan_chunks()
NCH = len(CHUNKS)
S_RING, PV_RING = 5, 3
assert NCH % S_RING == 0 and NCH % PV_RING == 0
NPROJ = 6
NTR = 2
NUP = HT // 2
FOLD = [True] * NCH


def attention_and_ffn(nc, k, io, scratch):
    with ExitStack() as ctx:
        a = Alloc(nc, ctx, "at")
        wqkv = [a.sb(f"w{s}", [P, DC, HC]) for s in "qkv"]
        bias = [a.sb(f"b{s}", [P, HC]) for s in "qkv"]
        wo = a.sb("wo", [P, HC // P, D])
        wgT, wuT, wdT = a.sb("wgT", [P, DC, HID]), a.sb("wuT", [P, DC, HID]), a.sb("wdT", [P, HT, D])
        s_buf = [a.sb(f"s{i}", [P, CHUNK_CAP]) for i in range(S_RING)]
        pv_buf = [a.sb(f"pv{i}", [P, CHUNK_CAP]) for i in range(PV_RING)]
        q = [a.sb(f"q{i}", [P, H, QS]) for i in range(2)]
        kk = [a.sb(f"k{i}", [P, H, QS]) for i in range(2)]
        vv = [a.sb(f"v{i}", [P, H, C]) for i in range(2)]
        mx = [a.sb(f"m{i}", [P, H, QS]) for i in range(2)]
        mn = a.sb("mn", [P, H, QS])
        keep_max, keep_min = a.sb("keep_max", [P, H, QS]), a.sb("keep_min", [P, H, QS])
        xT = [a.sb(f"xT{i}", [P, DC, P]) for i in range(2)]
        x2 = a.sb("x2", [P, D])
        attn, attnT = a.sb("attn", [P, HC]), a.sb("attnT", [P, HC // P, P])
        gu_sb = a.sb("gu_sb", [P, NUP, 2, 2, P])
        hid = a.sb("hid", [P, NUP, 2, P])
        out_sb = a.sb("out_sb", [P, D])
        num, den = a.ps("num", [P, H, C]), a.ps("den", [P, H, C])
        proj = [a.ps(f"proj{i}") for i in range(2)]
        up_ps, misc = a.ps("up"), a.ps("misc")

        w_in, dequant, x2_in, y_out, padded = (a.sem(s) for s in ("w_in", "dequant", "x2_in", "y_out", "padded"))
        xT_in = [a.sem(f"xT_in{u}") for u in range(2)]
        proj_done, proj_out, qk_ready, max_step, mult_done, sub_done, exp_done, pv_done, fold_done = (
            a.sem(s) for s in ("proj_done", "proj_out", "qk_ready", "max_step", "mult", "sub", "exp", "pv", "fold"))
        num_done, den_done, recip_done, attn_done, turned, turned_out = (
            a.sem(s) for s in ("num_done", "den_done", "recip", "attn", "turned", "turned_out"))
        up_done, up_out, silu_done, hid_done, acc_done, y_ready, settled = (
            a.sem(s) for s in ("up_done", "up_out", "silu", "hid", "acc", "y_ready", "settled"))

        stage = [s_buf[i][:, 0:DC * HID].bitcast(I32) for i in range(3)]
        with nc.Block() as block:

            @block.sync
            def _(sp):
                for i, name in enumerate(("WqT", "WkT", "WvT")):
                    sp.dma_start(wqkv[i][:], io[name].rearrange("(c p) n -> p c n", p=P)).then_inc(w_in, 16)
                for i, name in enumerate(("bq", "bk", "bv")):
                    sp.dma_start(bias[i][:], io[name].partition_broadcast(P)).then_inc(w_in, 16)
                sp.dma_start(wo[:], io["Wo"].rearrange("(c p) n -> p c n", p=P)).then_inc(w_in, 16)
                for i, (name, c) in enumerate((("wgT", DC), ("wuT", DC), ("wdT", HT))):
                    sp.dma_start(stage[i].rearrange("p (c n) -> p c n", c=c),
                                 io[name].rearrange("(c p) n -> p c n", p=P)).then_inc(w_in, 16)

            @block.vector
            def _(dve):
                dve.wait_ge(w_in, 160)
                v = nc.vector
                for i, w in enumerate((wgT, wuT, wdT)):
                    v.tensor_scalar(w[:].rearrange("p c n -> p (c n)"), stage[i], 1.0 / 127.0, None,
                                    ALU.mult).then_inc(dequant, 1)
                for t in (q[0], q[1], kk[0], kk[1], mx[0], mx[1], mn):
                    v.memset(t[:], 0.0).then_inc(padded, 1)
                v.memset(keep_max[:], 0.0).then_inc(padded, 1)
                v.memset(keep_min[:], 0.0).then_inc(padded, 1)
                dve.wait_ge(padded, 9)
                v.memset(keep_max[:, :, 0], -3.0e38).then_inc(padded, 1)
                v.memset(keep_min[:, :, 0], 3.0e38).then_inc(padded, 1)
                dve.wait_ge(padded, 11)
                dve.wait_ge(dequant, 3)

        def tile_loop(eng, tile):
            tile(0, 0)
            tile(1, 1)
            with eng.Fori(1, NT // 2) as i:
                tile(i * 2, 0)
                tile(i * 2 + 1, 1)

        def first(t):
            return isinstance(t, int) and t == 0

        def row(ap, n, off, heads=H):
            return view(ap[:], [[2 * n[0], heads], [1, n[1]]], off)

        PROJ_AT, TURN_AT, ACC_AT = 2, 8, 10
        EVAC_AT, MAX_AT, ATTN_AT, OUT_AT = 6, 12, 2, 15
        TURN_OUT_AT = 11

        with nc.Block() as block:

            @block.sync
            def _(sp):
                def load(t, u):
                    if not isinstance(t, int) or t >= 2:
                        sp.wait_ge(up_done, (t - 1) * NUP)
                        settle(sp, settled)
                    sp.dma_start(xT[u][:].rearrange("p c t -> p (c t)"),
                                 scratch["xT"][bass.ds(t, 1)].rearrange("o p n -> (o p) n")).then_inc(xT_in[u], 16)

                def finish(t):
                    wait(sp, y_ready, t)
                    settle(sp, settled)
                    sp.dma_start(x2[:], tokens(scratch["x2"])[:, bass.ds(t, 1), :].rearrange("p o d -> p (o d)")
                                 ).then_inc(x2_in, 16)
                    sp.wait_ge(y_ready, t + 1)
                    settle(sp, settled)
                    sp.dma_start(tokens(io["out"])[:, bass.ds(t, 1), :].rearrange("p o d -> p (o d)"), out_sb[:]
                                 ).then_inc(y_out, 16)

                def tile(t, u):
                    load(t + 1, 1 - u)
                    if not first(t):
                        finish(t - 1)

                load(0, 0)
                tile_loop(sp, tile)
                finish(NT - 1)
                sp.wait_ge(y_out, 16 * NT)

            @block.gpsimd
            def _(pool):
                def tile(t, u):
                    pool.wait_ge(qk_ready, 4 * (t + 1))
                    for c, (groups, size) in enumerate(CHUNKS):
                        wait(pool, den_done, t * NCH + c + 1 - S_RING)
                        for d, n, off in groups:
                            ins = nc.gpsimd.tensor_tensor(view(s_buf[c % S_RING][:], [[2 * n, H], [n, 2], [1, n]], off),
                                                          view(q[u][:], [[QS, H], [1, 2], [1, n]], d),
                                                          view(kk[u][:], [[QS, H], [0, 2], [1, n]]), ALU.mult)
                        ins.then_inc(mult_done, 1)
                tile_loop(pool, tile)

            @block.scalar
            def _(act):
                def turn_out(t, r):
                    act.wait_ge(turned, t * NTR + r + 1)
                    nc.scalar.copy(attnT[:, 4 * r:4 * r + 4, :].rearrange("p c t -> p (c t)"), misc[:]
                                   ).then_inc(turned_out, 1)

                def tile(t, u):
                    for c, (groups, size) in enumerate(CHUNKS):
                        act.wait_ge(sub_done, t * NCH + c + 1)
                        nc.scalar.activation(s_buf[c % S_RING][:, 0:size], s_buf[c % S_RING][:, 0:size], ACT.Exp,
                                             scale=C ** -0.5).then_inc(exp_done, 1)
                        if c < NUP:
                            act.wait_ge(up_done, t * NUP + c + 1)
                            wait(act, hid_done, t)
                            nc.scalar.copy(gu_sb[:, c].rearrange("p s h t -> p (s h t)"), up_ps[:]).then_inc(up_out, 1)
                        if TURN_OUT_AT <= c < TURN_OUT_AT + NTR and not first(t):
                            turn_out(t - 1, c - TURN_OUT_AT)
                    act.wait_ge(up_out, (t + 1) * NUP)
                    wait(act, acc_done, t)
                    nc.scalar.activation(hid[:], gu_sb[:, :, 0], ACT.Silu).then_inc(silu_done, 1)

                tile_loop(act, tile)
                for r in range(NTR):
                    turn_out(NT - 1, r)

            @block.vector
            def _(dve):
                v = nc.vector

                def subtract(t, u, c):
                    dve.wait_ge(mult_done, t * NCH + c + 1)
                    for d, n, off in CHUNKS[c][0]:
                        x = view(s_buf[c % S_RING][:], [[2 * n, H], [n, 2], [1, n]], off)
                        ins = v.tensor_tensor(x, x, view(mx[u][:], [[QS, H], [1, 2], [1, n]], d), ALU.subtract)
                    ins.then_inc(sub_done, 1)

                def times_v(t, u, c):
                    dve.wait_ge(exp_done, t * NCH + c + 1)
                    wait(dve, num_done, t * NCH + c + 1 - PV_RING)
                    for d, n, off in CHUNKS[c][0]:
                        ins = v.tensor_tensor(view(pv_buf[c % PV_RING][:], [[2 * n, H], [n, 2], [1, n]], off),
                                              view(s_buf[c % S_RING][:], [[2 * n, H], [n, 2], [1, n]], off),
                                              view(vv[u][:], [[C, H], [0, 2], [1, n]]), ALU.mult)
                    ins.then_inc(pv_done, 1)

                def fold(t, c):
                    if not FOLD[c]:
                        return
                    dve.wait_ge(pv_done, t * NCH + c + 1)
                    for buf in (pv_buf[c % PV_RING], s_buf[c % S_RING]):
                        for d, n, off in CHUNKS[c][0]:
                            x = row(buf, (n, n - 1), off + 1)
                            ins = v.tensor_tensor(x, x, row(buf, (n, n - 1), off + n), ALU.add)
                    ins.then_inc(fold_done, 1)

                def evacuate(t, u, b):
                    dve.wait_ge(proj_done, t * NPROJ + b + 1)
                    which, half = b // 2, b % 2
                    dst = (q, kk, vv)[which][u]
                    heads = slice(8 * half, 8 * half + 8)
                    if which < 2:
                        wait(dve, mult_done, (t - 1) * NCH)
                    else:
                        wait(dve, pv_done, (t - 1) * NCH)
                    ins = v.tensor_tensor(dst[:, heads, 0:C], proj[b % 2][:].rearrange("p (h c) -> p h c", c=C),
                                          bias[which][:, half * 512:half * 512 + 512].rearrange(
                                              "p (h c) -> p h c", c=C), ALU.add)
                    ins.then_inc(proj_out, 1)
                    if which < 2:
                        dve.wait_ge(proj_out, t * NPROJ + b + 1)
                        v.sem_inc(qk_ready, 1)

                def maxima(t, u):
                    flat = lambda x: x[:].rearrange("p h c -> p (h c)")
                    wait(dve, sub_done, (t - 1) * NCH)
                    dve.wait_ge(proj_out, t * NPROJ + 4)
                    v.tensor_tensor_scan(flat(mx[u]), flat(keep_max), flat(kk[u]), 0.0, ALU.add, ALU.max
                                         ).then_inc(max_step, 1)
                    v.tensor_tensor_scan(flat(mn), flat(keep_min), flat(kk[u]), 0.0, ALU.add, ALU.min
                                         ).then_inc(max_step, 1)
                    dve.wait_ge(max_step, t * 5 + 2)
                    v.tensor_tensor(mx[u][:], mx[u][:], q[u][:], ALU.mult).then_inc(max_step, 1)
                    v.tensor_tensor(mn[:], mn[:], q[u][:], ALU.mult).then_inc(max_step, 1)
                    dve.wait_ge(max_step, t * 5 + 4)
                    v.tensor_tensor(mx[u][:], mx[u][:], mn[:], ALU.max).then_inc(max_step, 1)
                    dve.wait_ge(max_step, t * 5 + 5)

                def divide(t):
                    dve.wait_ge(den_done, (t + 1) * NCH)
                    wait(dve, turned, t * NTR)
                    v.reciprocal(attn[:], den[:].rearrange("p h c -> p (h c)")).then_inc(recip_done, 1)
                    dve.wait_ge(recip_done, t + 1)
                    v.tensor_tensor(attn[:], num[:].rearrange("p h c -> p (h c)"), attn[:], ALU.mult
                                    ).then_inc(attn_done, 1)

                def output(t):
                    dve.wait_ge(acc_done, t + 1)
                    dve.wait_ge(x2_in, 16 * (t + 1))
                    wait(dve, y_out, 16 * t)
                    v.tensor_tensor(out_sb[:], misc[:, 0:D], x2[:], ALU.add).then_inc(y_ready, 1)

                def tile(t, u):
                    for s in range(NCH + 3):
                        if s < NCH:
                            subtract(t, u, s)
                        if s >= 3:
                            fold(t, s - 3)
                        if 2 <= s < NCH + 2:
                            times_v(t, u, s - 2)
                        if s == ATTN_AT and not first(t):
                            divide(t - 1)
                        if EVAC_AT <= s < EVAC_AT + NPROJ:
                            evacuate(t + 1, 1 - u, s - EVAC_AT)
                        if s == MAX_AT:
                            maxima(t + 1, 1 - u)
                        if s == OUT_AT and not first(t):
                            output(t - 1)
                    dve.wait_ge(silu_done, t + 1)
                    v.tensor_tensor(hid[:], hid[:], gu_sb[:, :, 1], ALU.mult).then_inc(hid_done, 1)

                for b in range(NPROJ):
                    evacuate(0, 0, b)
                maxima(0, 0)
                tile_loop(dve, tile)
                divide(NT - 1)
                output(NT - 1)

            @block.tensor
            def _(pe):
                def project(t, u, b):
                    pe.wait_ge(xT_in[u], 8 * (t - u) + 16)
                    wait(pe, proj_out, t * NPROJ + b - 1)
                    which, half = b // 2, b % 2
                    for c in range(DC):
                        ins = nc.tensor.matmul(proj[b % 2][:], xT[u][:, c, :],
                                               wqkv[which][:, c, half * 512:half * 512 + 512],
                                               start=(c == 0), stop=(c == DC - 1))
                    ins.then_inc(proj_done, 1)

                def up(t, u, r):
                    pe.wait_ge(xT_in[u], 8 * (t - u) + 16)
                    wait(pe, up_out, t * NUP + r)
                    for s, w in enumerate((wgT, wuT)):
                        for h in range(2):
                            m = 2 * r + h
                            for c in range(DC):
                                ins = nc.tensor.matmul(up_ps[:, (2 * s + h) * P:(2 * s + h + 1) * P],
                                                       w[:, c, m * P:(m + 1) * P], xT[u][:, c, :],
                                                       start=(c == 0), stop=(c == DC - 1))
                    ins.then_inc(up_done, 1)

                def sums(t, c):
                    if FOLD[c]:
                        pe.wait_ge(fold_done, t * sum(FOLD) + sum(FOLD[:c + 1]))
                    else:
                        pe.wait_ge(pv_done, t * NCH + c + 1)
                    for dst, buf, done in ((num, pv_buf[c % PV_RING], num_done), (den, s_buf[c % S_RING], den_done)):
                        for d, n, off in CHUNKS[c][0]:
                            for half in range(2):
                                heads = slice(8 * half, 8 * half + 8)
                                ins = nc.tensor.matmul(dst[:, heads, d:C], k.ident[:],
                                                       row(buf, (n, n), off + 16 * n * half, 8),
                                                       start=(d == 0), stop=False, skip_group_check=True)
                                if not FOLD[c]:
                                    ins = nc.tensor.matmul(dst[:, heads, d + 1:C], k.ident[:],
                                                           row(buf, (n, n - 1), off + 16 * n * half + n, 8),
                                                           start=False, stop=False, skip_group_check=True)
                        ins.then_inc(done, 1)

                def turn(t, r):
                    pe.wait_ge(attn_done, t + 1)
                    wait(pe, turned_out, t * NTR + r)
                    if r == 0:
                        wait(pe, y_ready, t)
                    for c in range(4):
                        ins = nc.tensor.transpose(misc[:, c * P:(c + 1) * P],
                                                  attn[:, (4 * r + c) * P:(4 * r + c + 1) * P], k.ident[:])
                    ins.then_inc(turned, 1)

                def down(t):
                    pe.wait_ge(turned_out, (t + 1) * NTR)
                    pe.wait_ge(hid_done, t + 1)
                    for c in range(HC // P):
                        nc.tensor.matmul(misc[:, 0:D], attnT[:, c, :], wo[:, c, :], start=(c == 0), stop=False)
                    for m in range(HT):
                        ins = nc.tensor.matmul(misc[:, 0:D], hid[:, m // 2, m % 2, :], wdT[:, m, :], start=False,
                                               stop=(m == HT - 1))
                    ins.then_inc(acc_done, 1)

                def tile(t, u):
                    up(t, u, 0)
                    wait(pe, attn_done, t)
                    for c in range(NCH):
                        sums(t, c)
                        if c + 1 < NUP:
                            up(t, u, c + 1)
                        if PROJ_AT <= c < PROJ_AT + NPROJ:
                            project(t + 1, 1 - u, c - PROJ_AT)
                        if TURN_AT <= c < TURN_AT + NTR and not first(t):
                            turn(t - 1, c - TURN_AT)
                        if c == ACC_AT and not first(t):
                            down(t - 1)

                for b in range(NPROJ):
                    project(0, 0, b)
                tile_loop(pe, tile)
                for r in range(NTR):
                    turn(NT - 1, r)
                down(NT - 1)


class Shared:
    pass


def build(nc, io, scratch):
    k = Shared()
    with ExitStack() as outer:
        a = Alloc(nc, outer, "k")
        make_constants(nc, a, k)
        with ExitStack() as early:
            b = Alloc(nc, early, "e")
            k.x, k.xn = b.sb("x", [P, NT, D]), b.sb("xn", [P, NT, D])
            k.slot = b.sb("slot", [P, NT, 8], I32)
            k.choice_w = b.sb("choice_w", [P, TOPK, NT])
            k.weight_row = b.sb("weight_row", [P, SLOT_BLOCKS], I32)
            k.slot_tok = b.sb("slot_tok", [P, SLOT_BLOCKS], I32)
            with ExitStack() as turned:
                c = Alloc(nc, turned, "t")
                k.xnT = c.sb("xnT", [P, DC, T])
                k.score, k.gate_bias = c.sb("score", [P, NT, E]), c.sb("gate_bias", [P, E])
                normalise_and_score(nc, k, io, scratch)
                route(nc, k, io, scratch)
                recurrence_and_shared(nc, k, io, scratch)
            routed_experts(nc, k, io, scratch)
            combine(nc, k, io, scratch)
        attention_and_ffn(nc, k, io, scratch)


def kernel(**inputs):
    import numpy as np
    import concourse.bacc as bacc
    from concourse.bass_utils import run_bass_kernel_spmd

    g = {n: np.asarray(v) for n, v in inputs.items()}
    f0, f1, s0, a1 = "L0_ffn_", "L1_ffn_", "L0_attn_", "L1_attn_"

    def halves(w):
        return w.reshape(E, INTER, DC, P).transpose(0, 3, 2, 1).reshape(E * P, DC * INTER)

    arrays = {
        "u": g[s0 + "u"].reshape(T, D),
        "log_neg_real": g[s0 + "log_neg_real"].reshape(NS, 1), "imag": g[s0 + "imag"].reshape(NS, 1),
        "bT": g[s0 + "B_mat"].T, "cT": g[s0 + "C_mat"].T,
        "D": g[s0 + "D"], "gamma": g[s0 + "gamma"], "beta": g[s0 + "beta"],
        "gate_wT": g[f0 + "gate_w"].T, "gate_bias": g[f0 + "gate_bias"],
        "experts": np.concatenate([halves(g[f0 + "eg_w"]), halves(g[f0 + "eu_w"]),
                                   g[f0 + "ed_w"].transpose(0, 2, 1).reshape(E * P, D)], axis=1),
        "sgT": g[f0 + "sg_w"].T, "suT": g[f0 + "su_w"].T, "sdT": g[f0 + "sd_w"].T,
        "WqT": g[a1 + "Wq"], "WkT": g[a1 + "Wk"], "WvT": g[a1 + "Wv"], "Wo": g[a1 + "Wo"],
        "bq": g[a1 + "bq"], "bk": g[a1 + "bk"], "bv": g[a1 + "bv"], "bo": g[a1 + "bo"],
        "wgT": g[f1 + "w_gate"].T, "wuT": g[f1 + "w_up"].T, "wdT": g[f1 + "w_down"].T,
    }
    arrays = {n: np.ascontiguousarray(v) for n, v in arrays.items()}
    nc = bacc.Bacc("TRN2", target_bir_lowering=False, num_devices=1)
    io = {n: nc.dram_tensor(n, v.shape, mybir.dt.from_np(v.dtype), kind="ExternalInput").ap()
          for n, v in arrays.items()}
    io["out"] = nc.dram_tensor("out", (T, D), F32, kind="ExternalOutput").ap()
    scratch = {n: nc.dram_tensor(n, shape, F32).ap() for n, shape in (
        ("xn", (T, D)), ("slot_token", (SLOTS, 1)), ("slot_out", (SLOTS, D)), ("x2", (T, D)),
        ("xT", (NT + 1, P, D)))}
    build(nc, io, scratch)
    r = run_bass_kernel_spmd(nc, [arrays], core_ids=[0])
    return r.results[0]["out"].reshape(BATCH, SEQ, D)
```

```python
from contextlib import ExitStack

import concourse.bass as bass
from concourse import mybir

ALU = mybir.AluOpType
ACT = mybir.ActivationFunctionType
AX = mybir.AxisListType
F32 = mybir.dt.float32
I32 = mybir.dt.int32

P = 128
BATCH, SEQ, D = 4, 1024, 256
T = BATCH * SEQ
NT = T // P
DC = D // P
NS = 64
E, GROUPS, TOPG, TOPK = 64, 8, 4, 6
EG = E // GROUPS
INTER = 128
NSH = 2
SLOT_BLOCKS = T * TOPK // P + E
SLOTS = SLOT_BLOCKS * P
H, C = 16, 64
HC = H * C
HID = 768
HT = HID // P
QS = C + 4
EPS = 1e-5
LOG_SEQ = 10
TWO_PI_HI, TWO_PI_MID, TWO_PI_LO = 6.28125, 0.0019350051879882812, 3.019916050561733e-07
ROUND_MAGIC = 12582912.0
INV_TWO_PI = 0.15915494309189535


def view(ap, dims, offset=0):
    return bass.AP(tensor=ap.tensor, offset=ap.offset + offset, ap=[list(ap.ap[0])] + [list(d) for d in dims])


def wait(eng, sem, value):
    if isinstance(value, int) and value <= 0:
        return
    eng.wait_ge(sem, value)


def settle(eng, sem):
    eng.sem_inc(sem, 1)


class Chain:

    def __init__(self, eng, sem):
        self.eng, self.sem, self.n = eng, sem, 0

    def __call__(self, ins):
        self.mark(ins)
        self.join()

    def mark(self, ins):
        self.n += 1
        ins.then_inc(self.sem, 1)

    def join(self):
        self.eng.wait_ge(self.sem, self.n)


class Alloc:
    def __init__(self, nc, ctx, tag):
        self.nc, self.ctx, self.tag = nc, ctx, tag

    def sb(self, name, shape, dt=F32):
        return self.ctx.enter_context(self.nc.sbuf_tensor(f"{self.tag}_{name}", shape, dt))

    def ps(self, name, shape=(P, 512), dt=F32):
        return self.ctx.enter_context(self.nc.psum_tensor(f"{self.tag}_{name}", list(shape), dt))

    def sem(self, name):
        return self.ctx.enter_context(self.nc.semaphore(f"{self.tag}_{name}"))


def tokens(ap):
    return ap.rearrange("(n p) d -> p n d", p=P)


def make_constants(nc, a, k):
    k.ident = a.sb("ident", [P, P])
    k.upper = a.sb("upper", [P, P])
    k.ones = a.sb("ones", [P, P])
    k.tri8 = a.sb("tri8", [P, GROUPS, GROUPS])
    k.top_half = a.sb("top_half", [P, 1])
    k.iota_p = a.sb("iota_p", [P, 2])
    k.tokid = a.sb("tokid", [P, NT])
    k.minus_half = a.sb("minus_half", [P, NT])
    s = a.sem("const")
    with nc.Block() as block:

        @block.gpsimd
        def _(pool):
            c = Chain(pool, s)
            c.mark(nc.gpsimd.memset(k.ident[:], 0.0))
            c.mark(nc.gpsimd.memset(k.upper[:], 1.0))
            c.mark(nc.gpsimd.memset(k.ones[:], 1.0))
            c.mark(nc.gpsimd.memset(k.tri8[:], 1.0))
            c.mark(nc.gpsimd.memset(k.top_half[:], 1.0))
            c.mark(nc.gpsimd.memset(k.minus_half[:], -0.5))
            c.join()
            c.mark(nc.gpsimd.affine_select(out=k.ident[:], in_=k.ident[:], compare_op=ALU.not_equal, fill=1.0,
                                           base=0, pattern=[[-1, P]], channel_multiplier=1))
            c.mark(nc.gpsimd.affine_select(out=k.upper[:], in_=k.upper[:], compare_op=ALU.is_gt, fill=0.0,
                                           base=0, pattern=[[1, P]], channel_multiplier=-1))
            c.mark(nc.gpsimd.affine_select(out=k.tri8[:], in_=k.tri8[:], compare_op=ALU.is_gt, fill=0.0,
                                           base=0, pattern=[[1, GROUPS], [-1, GROUPS]], channel_multiplier=0))
            c.mark(nc.gpsimd.affine_select(out=k.top_half[:], in_=k.top_half[:], compare_op=ALU.is_gt, fill=0.0,
                                           base=NS, pattern=[[0, 1]], channel_multiplier=-1))
            c.mark(nc.gpsimd.iota(k.iota_p[:], [[P, 2]], base=0, channel_multiplier=1,
                                  allow_small_or_imprecise_dtypes=True))
            c.mark(nc.gpsimd.iota(k.tokid[:], [[P, NT]], base=0, channel_multiplier=1,
                                  allow_small_or_imprecise_dtypes=True))
            c.join()


def normalise_and_score(nc, k, io, scratch):
    with ExitStack() as ctx:
        a = Alloc(nc, ctx, "ln")
        gate_wT = a.sb("gate_wT", [P, DC, E])
        stats = a.sb("stats", [P, NT, 6])
        mv = a.sb("mv", [P, NT, 2])
        rstd = a.sb("rstd", [P, NT])
        tr = [a.ps(f"tr{i}", [P, DC, P]) for i in range(2)]
        logits = a.ps("logits", [P, NT, E])
        w_in, moments, pow_done, xn_done = (a.sem(s) for s in ("w_in", "moments", "pow", "xn"))
        x_in = [a.sem(f"x_in{q}") for q in range(4)]
        turned, evacuated, logit_done, score_done, xn_out = (
            a.sem(s) for s in ("turned", "evac", "logit", "score", "xn_out"))
        dve_step, pool_step = a.sem("dve"), a.sem("pool")
        PER = NT // 4
        with nc.Block() as block:

            @block.sync
            def _(sp):
                for q in range(4):
                    sp.dma_start(k.x[:, q * PER:(q + 1) * PER, :],
                                 tokens(io["u"])[:, q * PER:(q + 1) * PER, :]).then_inc(x_in[q], 16)
                sp.dma_start(gate_wT[:], io["gate_wT"].rearrange("(c p) e -> p c e", p=P)).then_inc(w_in, 16)
                sp.dma_start(k.gate_bias[:], io["gate_bias"].partition_broadcast(P)).then_inc(w_in, 16)
                for q in range(4):
                    sp.wait_ge(xn_done, (q + 1) * PER)
                    sp.dma_start(tokens(scratch["xn"])[:, q * PER:(q + 1) * PER, :],
                                 k.xn[:, q * PER:(q + 1) * PER, :]).then_inc(xn_out, 16)
                sp.wait_ge(xn_out, 64)

            @block.vector
            def _(dve):
                c = Chain(dve, dve_step)
                for n in range(NT):
                    if n % PER == 0:
                        dve.wait_ge(x_in[n // PER], 16)
                    c.mark(nc.vector.bn_stats(stats[:, n, :], k.x[:, n, :]))
                c.join()
                for n in range(NT):
                    nc.vector.bn_aggr(mv[:, n, :], stats[:, n, :]).then_inc(moments, 1)
                dve.wait_ge(pow_done, 1)
                for n in range(NT):
                    nc.vector.tensor_scalar(k.xn[:, n, :], k.x[:, n, :], mv[:, n, 0:1], rstd[:, n:n + 1],
                                            ALU.subtract, ALU.mult).then_inc(xn_done, 1)

            @block.gpsimd
            def _(pool):
                c = Chain(pool, pool_step)
                pool.wait_ge(moments, NT)
                c(nc.gpsimd.tensor_scalar(rstd[:], mv[:, :, 1], EPS, None, ALU.add))
                nc.gpsimd.tensor_tensor(rstd[:], rstd[:], k.minus_half[:], ALU.pow).then_inc(pow_done, 1)

            @block.tensor
            def _(pe):
                def score(n):
                    pe.wait_ge(evacuated, n + 1)
                    for c in range(DC):
                        ins = nc.tensor.matmul(logits[:, n, :], k.xnT[:, c, n * P:(n + 1) * P], gate_wT[:, c, :],
                                               start=(c == 0), stop=(c == DC - 1), skip_group_check=True)
                    ins.then_inc(logit_done, 1)

                pe.wait_ge(w_in, 32)
                for n in range(NT):
                    pe.wait_ge(xn_done, n + 1)
                    wait(pe, evacuated, n - 1)
                    for c in range(DC):
                        ins = nc.tensor.transpose(tr[n % 2][:, c, :], k.xn[:, n, c * P:(c + 1) * P], k.ident[:])
                    ins.then_inc(turned, 1)
                    if n:
                        score(n - 1)
                score(NT - 1)

            @block.scalar
            def _(act):
                for n in range(NT):
                    act.wait_ge(turned, n + 1)
                    nc.scalar.copy(k.xnT[:, :, n * P:(n + 1) * P], tr[n % 2][:]).then_inc(evacuated, 1)
                for q in range(4):
                    act.wait_ge(logit_done, NT)
                    nc.scalar.activation(k.score[:, q * 8:(q + 1) * 8, :], logits[:, q * 8:(q + 1) * 8, :],
                                         ACT.Sigmoid).then_inc(score_done, 1)
                act.wait_ge(score_done, 4)


def route(nc, k, io, scratch):
    with ExitStack() as ctx:
        a = Alloc(nc, ctx, "rt")
        gm = a.sb("gm", [P, NT, GROUPS])
        rank = a.sb("rank", [P, NT, GROUPS])
        cmpa = a.sb("cmpa", [P, NT * E])
        cmpb = a.sb("cmpb", [P, NT * E])
        keep = a.sb("keep", [P, NT * E])
        sel = a.sb("sel", [P, NT, E])
        comb = a.sb("comb", [P, NT, E])
        key = a.sb("key", [P, NT, E])
        tot = a.sb("tot", [P, E, NT])
        excl = a.sb("excl", [P, E, NT])
        keep_t = a.sb("keep_t", [P, E, NT])
        top8 = a.sb("top8", [P, NT, 8])
        small = a.sb("small", [P, NT])
        blocks_i = a.sb("blocks_i", [P, E], I32)
        blocks = a.sb("blocks", [P, E])
        ends = a.sb("ends", [P, E])
        base = a.sb("base", [P, E])
        cmpe = a.sb("cmpe", [P, 2, E])
        bexp = a.sb("bexp", [P, 2])
        diag = a.sb("diag", [P, 2, P])
        zeros = a.sb("zeros", [P, SLOTS // P])
        tab = a.sb("tab", [P, 2, P])
        cum = a.ps("cum", [P, NT, E])
        all_ = a.ps("all", [P, NT, E])
        masks, sel_done, cum_done, slots_done, zeroed = (a.sem(s) for s in ("masks", "sel", "cum", "slots", "zeroed"))
        scattered, copied, tab_in, diag_done, bexp_done, widx_done = (
            a.sem(s) for s in ("scattered", "copied", "tab_in", "diag", "bexp", "widx"))
        turned, dve_step = a.sem("turned"), a.sem("dve")

        with nc.Block() as block:

            @block.gpsimd
            def _(pool):
                nc.gpsimd.memset(keep[:], 1.0).then_inc(masks, 1)
                nc.gpsimd.memset(keep_t[:], 1.0).then_inc(masks, 1)
                nc.gpsimd.memset(zeros[:], 0.0).then_inc(masks, 1)
                pool.wait_ge(masks, 3)
                nc.gpsimd.memset(view(keep[:], [[E, NT]]), 0.0).then_inc(masks, 1)
                nc.gpsimd.memset(keep_t[:, :, 0], 0.0).then_inc(masks, 1)
                pool.wait_ge(zeroed, 16)
                pool.wait_ge(slots_done, 1)
                for n in range(NT):
                    for j in range(TOPK):
                        nc.gpsimd.indirect_dma_start(
                            scratch["slot_token"], bass.IndirectOffsetOnAxis(ap=k.slot[:, n, j:j + 1], axis=0),
                            k.tokid[:, n:n + 1], None).then_inc(scattered, 16)
                pool.wait_ge(scattered, 16 * NT * TOPK)

            @block.sync
            def _(sp):
                sp.wait_ge(masks, 3)
                sp.dma_start(scratch["slot_token"].rearrange("(p s) o -> p (s o)", p=P), zeros[:]).then_inc(zeroed, 16)
                sp.wait_ge(zeroed, 16)
                sp.wait_ge(scattered, 16 * NT * TOPK)
                sp.dma_start(tab[:], scratch["slot_token"].rearrange("(c b s) o -> b c (s o)", c=2, s=P)
                             ).then_inc(tab_in, 16)

            @block.vector
            def _(dve):
                c = Chain(dve, dve_step)
                v = nc.vector
                sc = k.score
                c(v.tensor_tensor(sc[:], sc[:], view(k.gate_bias[:], [[0, NT], [1, E]]), ALU.add))
                c(v.tensor_reduce(gm[:], sc[:].rearrange("p n (g e) -> p n g e", g=GROUPS), AX.X, ALU.max))
                other = view(gm[:], [[GROUPS, NT], [0, GROUPS], [1, GROUPS]])
                own = view(gm[:], [[GROUPS, NT], [1, GROUPS], [0, GROUPS]])
                a4 = view(cmpa[:], [[E, NT], [GROUPS, GROUPS], [1, GROUPS]])
                b4 = view(cmpb[:], [[E, NT], [GROUPS, GROUPS], [1, GROUPS]])
                c.mark(v.tensor_tensor(a4, other, own, ALU.is_gt))
                c(v.tensor_tensor(b4, other, own, ALU.is_equal))
                c(v.tensor_tensor(b4, b4, view(k.tri8[:], [[0, NT], [GROUPS, GROUPS], [1, GROUPS]]), ALU.mult))
                c(v.tensor_tensor(cmpa[:], cmpa[:], cmpb[:], ALU.add))
                c(v.tensor_reduce(rank[:], a4, AX.X, ALU.add))
                c(v.tensor_scalar(rank[:], rank[:], float(TOPG), None, ALU.is_lt))
                ms = key
                c(v.tensor_tensor(view(ms[:], [[EG, NT * GROUPS], [1, EG]]), view(sc[:], [[EG, NT * GROUPS], [1, EG]]),
                                  view(rank[:], [[1, NT * GROUPS], [0, EG]]), ALU.mult))
                for n in range(NT):
                    c.mark(v.max(top8[:, n, :], ms[:, n, :]))
                c.join()
                thr = view(top8[:], [[8, NT], [0, E]], TOPK - 1)
                gt = view(cmpa[:], [[E, NT], [1, E]])
                eq = view(cmpb[:], [[E, NT], [1, E]])
                c.mark(v.tensor_tensor(gt, ms[:], thr, ALU.is_gt))
                c(v.tensor_tensor(eq, ms[:], thr, ALU.is_equal))
                c.mark(v.tensor_reduce(small[:], gt, AX.X, ALU.add))
                dve.wait_ge(masks, 5)
                c(v.tensor_tensor_scan(comb[:].rearrange("p n e -> p (n e)"), keep[:], cmpb[:], 0.0, ALU.mult, ALU.add))
                c(v.tensor_scalar(small[:], small[:], -1.0, float(TOPK), ALU.mult, ALU.add))
                c(v.tensor_tensor(comb[:], comb[:], view(small[:], [[1, NT], [0, E]]), ALU.is_le))
                c(v.tensor_tensor(comb[:], comb[:], eq, ALU.mult))
                c(v.tensor_tensor(sel[:], comb[:], gt, ALU.add))
                c(v.tensor_tensor(comb[:], sel[:], ms[:], ALU.mult))
                c(v.tensor_reduce(small[:], comb[:], AX.X, ALU.add))
                c(v.tensor_scalar(small[:], small[:], 1e-8, None, ALU.add))
                c(v.reciprocal(small[:], small[:]))
                v.tensor_tensor(comb[:], comb[:], view(small[:], [[1, NT], [0, E]]), ALU.mult).then_inc(sel_done, 1)
                dve.wait_ge(sel_done, 1)
                dve.wait_ge(cum_done, 2)
                c(v.tensor_copy(tot[:], all_[:].rearrange("p n e -> p e n")))
                c(v.tensor_tensor_scan(excl[:].rearrange("p e n -> p (e n)"), keep_t[:].rearrange("p e n -> p (e n)"),
                                       tot[:].rearrange("p e n -> p (e n)"), 0.0, ALU.mult, ALU.add))
                c(v.tensor_scalar(blocks_i[:], excl[:, :, NT - 1], float(P - 1), None, ALU.add))
                c(v.tensor_scalar(blocks_i[:], blocks_i[:], P.bit_length() - 1, None, ALU.logical_shift_right))
                c(v.tensor_copy(blocks[:], blocks_i[:]))
                c(v.tensor_tensor_scan(ends[:], k.ones[:, 0:E], blocks[:], 0.0, ALU.mult, ALU.add))
                c(v.tensor_tensor(base[:], ends[:], blocks[:], ALU.subtract))
                c(v.tensor_scalar(base[:], base[:], float(P), 1.0, ALU.mult, ALU.add))
                c(v.tensor_tensor(excl[:], excl[:], tot[:], ALU.subtract))
                c(v.tensor_tensor(key[:], cum[:], excl[:].rearrange("p e n -> p n e"), ALU.add))
                c(v.tensor_tensor(key[:], key[:], view(base[:], [[0, NT], [1, E]]), ALU.add))
                c(v.tensor_tensor(key[:], key[:], sel[:], ALU.mult))
                for n in range(NT):
                    c.mark(v.max(top8[:, n, :], key[:, n, :]))
                c.join()
                v.tensor_scalar(k.slot[:], top8[:], -1.0, None, ALU.add).then_inc(slots_done, 1)
                for h in range(2):
                    c.mark(v.tensor_scalar(cmpe[:, h, :], ends[:], k.iota_p[:, h:h + 1], None, ALU.is_le))
                c.join()
                c(v.tensor_reduce(bexp[:], cmpe[:], AX.X, ALU.add))
                c(v.tensor_scalar(bexp[:], bexp[:], float(E - 1), None, ALU.min))
                for h in range(2):
                    v.tensor_scalar(diag[:, h, :], k.ident[:], bexp[:, h:h + 1], None, ALU.mult).then_inc(diag_done, 1)
                dve.wait_ge(bexp_done, 1)
                v.tensor_scalar(k.weight_row[:], all_[:].rearrange("p n e -> p (n e)")[:, 0:2 * P], float(P),
                                k.iota_p[:, 0:1], ALU.mult, ALU.add).then_inc(widx_done, 1)
                for j in range(TOPK):
                    c(v.tensor_tensor(gt, key[:], view(top8[:], [[8, NT], [0, E]], j), ALU.is_equal))
                    c(v.tensor_tensor(gt, gt, comb[:], ALU.mult))
                    c(v.tensor_reduce(k.choice_w[:, j, :], gt, AX.X, ALU.add))
                dve.wait_ge(widx_done, 1)
                dve.wait_ge(turned, 2)
                c(v.tensor_copy(k.slot_tok[:], all_[:].rearrange("p n e -> p (n e)")[:, 512:512 + 2 * P]))

            @block.tensor
            def _(pe):
                pe.wait_ge(sel_done, 1)
                for q in range(4):
                    ins = nc.tensor.matmul(cum[:, q * 8:(q + 1) * 8, :], k.upper[:], sel[:, q * 8:(q + 1) * 8, :],
                                           start=True, stop=True)
                ins.then_inc(cum_done, 1)
                for q in range(4):
                    ins = nc.tensor.matmul(all_[:, q * 8:(q + 1) * 8, :], k.ones[:], sel[:, q * 8:(q + 1) * 8, :],
                                           start=True, stop=True)
                ins.then_inc(cum_done, 1)
                pe.wait_ge(diag_done, 2)
                ins = nc.tensor.matmul(all_[:].rearrange("p n e -> p (n e)")[:, 0:2 * P], k.ones[:],
                                       diag[:].rearrange("p c b -> p (c b)"), start=True, stop=True)
                ins.then_inc(bexp_done, 1)
                pe.wait_ge(tab_in, 16)
                for h in range(2):
                    nc.tensor.transpose(all_[:].rearrange("p n e -> p (n e)")[:, 512 + h * P:512 + (h + 1) * P],
                                        tab[:, h, :], k.ident[:]).then_inc(turned, 1)


def recurrence_and_shared(nc, k, io, scratch):
    with ExitStack() as ctx:
        a = Alloc(nc, ctx, "ssm")
        bT = a.sb("bT", [P, DC, P])
        cT = a.sb("cT", [P, D])
        sgT, suT = a.sb("sgT", [P, DC, NSH * P]), a.sb("suT", [P, DC, NSH * P])
        sdT = a.sb("sdT", [P, NSH, D])
        vec = a.sb("vec", [P, 2])
        d1, gamma, beta = a.sb("d1", [P, D]), a.sb("gamma", [P, D]), a.sb("beta", [P, D])
        sv = a.sb("sv", [P, 24])
        ang, kk, sn, cs = (a.sb(s, [P, LOG_SEQ]) for s in ("ang", "kk", "sn", "cs"))
        ct, st = a.sb("ct", [P, SEQ]), a.sb("st", [P, SEQ])
        wt, rot = a.sb("wt", [P, SEQ]), a.sb("rot", [P, SEQ])
        tmp = a.sb("tmp", [P, SEQ // 2])
        bu, hs = a.sb("bu", [P, 2, SEQ]), a.sb("hs", [P, 2, SEQ])
        xs = a.sb("xs", [P, NT, D])
        stats, mv, rstd = a.sb("stats", [P, NT, 6]), a.sb("mv", [P, NT, 2]), a.sb("rstd", [P, NT])
        sg, sh = a.sb("sg", [P, 2, 512]), a.sb("sh", [P, 2, NSH, 512])
        z = [a.ps(f"z{i}") for i in range(2)]
        y = [a.ps(f"y{i}", [P, D]) for i in range(2)]
        gps, ups = a.ps("gps"), a.ps("ups")
        w_in, moments = a.sem("w_in"), a.sem("moments")
        dve_step, act_step, pool_step = a.sem("dve"), a.sem("act"), a.sem("pool")
        e_done, ang_done, trig_done = a.sem("e"), a.sem("ang"), a.sem("trig")
        z_done, z_free, hs_done, y_done = (a.sem(s) for s in ("z_done", "z_free", "hs_done", "y_done"))
        u_done, skip_done, norm_done, pow_done = (a.sem(s) for s in ("u_done", "skip", "norm", "pow"))
        g_done, silu_done, sh_done, sy_done, sy_free = (
            a.sem(s) for s in ("g_done", "silu", "sh_done", "sy_done", "sy_free"))
        NW = 11
        HALF = SEQ // 512
        with nc.Block() as block:

            @block.sync
            def _(sp):
                for h in range(2):
                    half = slice(h * NS, (h + 1) * NS)
                    sp.dma_start(vec[half, 0:1], io["log_neg_real"]).then_inc(w_in, 16)
                    sp.dma_start(vec[half, 1:2], io["imag"]).then_inc(w_in, 16)
                    sp.dma_start(cT[half, :], io["cT"]).then_inc(w_in, 16)
                    sp.dma_start(bT[:, :, half], io["bT"].rearrange("(c p) n -> p c n", p=P)).then_inc(w_in, 16)
                for dst, name in ((d1, "D"), (gamma, "gamma"), (beta, "beta")):
                    sp.dma_start(dst[:], io[name].partition_broadcast(P)).then_inc(w_in, 16)
                sp.dma_start(sgT[:], io["sgT"].rearrange("(c p) i -> p c i", p=P)).then_inc(w_in, 16)
                sp.dma_start(suT[:], io["suT"].rearrange("(c p) i -> p c i", p=P)).then_inc(w_in, 16)
                sp.dma_start(sdT[:], io["sdT"].rearrange("(c p) h -> p c h", p=P)).then_inc(w_in, 16)

            W_ALL = 16 * 14

            @block.scalar
            def _(act):
                act.wait_ge(w_in, W_ALL)
                c = Chain(act, act_step)
                c(nc.scalar.activation(sv[:, 0:1], vec[:, 0:1], ACT.Exp))
                nc.scalar.activation(sv[:, 1:2], sv[:, 0:1], ACT.Exp, scale=-1.0).then_inc(e_done, 1)
                act.wait_ge(ang_done, 1)
                c.mark(nc.scalar.activation(sn[:], ang[:], ACT.Sin))
                nc.scalar.activation(cs[:], kk[:], ACT.Sin).then_inc(trig_done, 1)
                act.wait_ge(act_step, 2)
                for q in range(T // 512):
                    for i in range(NSH):
                        n = q * NSH + i
                        act.wait_ge(g_done, n + 1)
                        wait(act, sh_done, n - 1)
                        nc.scalar.activation(sg[:, n % 2, :], gps[:], ACT.Silu).then_inc(silu_done, 1)

            @block.gpsimd
            def _(pool):
                pool.wait_ge(w_in, W_ALL)
                c = Chain(pool, pool_step)
                c(nc.gpsimd.tensor_scalar(d1[:], d1[:], 1.0, None, ALU.add))
                for n in range(NT):
                    nc.gpsimd.tensor_tensor(xs[:, n, :], k.xn[:, n, :], d1[:], ALU.mult).then_inc(skip_done, 1)
                for n in range(NT):
                    c.mark(nc.gpsimd.tensor_tensor(k.x[:, n, :], k.x[:, n, :], beta[:], ALU.add))
                c.join()
                pool.wait_ge(moments, NT)
                c(nc.gpsimd.tensor_scalar(rstd[:], mv[:, :, 1], EPS, None, ALU.add))
                nc.gpsimd.tensor_tensor(rstd[:], rstd[:], k.minus_half[:], ALU.pow).then_inc(pow_done, 1)

            @block.vector
            def _(dve):
                v = nc.vector
                c = Chain(dve, dve_step)
                dve.wait_ge(w_in, W_ALL)
                for m in range(LOG_SEQ):
                    c.mark(v.tensor_scalar(ang[:, m:m + 1], vec[:, 1:2], float(2 ** m), None, ALU.mult))
                c.join()
                c(v.tensor_scalar(kk[:], ang[:], INV_TWO_PI, ROUND_MAGIC, ALU.mult, ALU.add))
                c(v.tensor_scalar(kk[:], kk[:], ROUND_MAGIC, None, ALU.subtract))
                for part in (TWO_PI_HI, TWO_PI_MID, TWO_PI_LO):
                    c(v.scalar_tensor_tensor(out=ang[:], in0=kk[:], scalar=-part, in1=ang[:], op0=ALU.mult, op1=ALU.add))
                c(v.tensor_scalar(ang[:], ang[:], 3.1415925, -3.1415925, ALU.min, ALU.max))
                c(v.tensor_scalar(kk[:], ang[:], -1.0, None, ALU.mult))
                c(v.tensor_tensor(kk[:], kk[:], ang[:], ALU.min))
                v.tensor_scalar(kk[:], kk[:], 1.5707963267948966, None, ALU.add).then_inc(ang_done, 1)
                dve.wait_ge(e_done, 1)
                dve.wait_ge(trig_done, 1)
                dve.wait_ge(act_step, 2)
                e, r, w = sv[:, 0:1], sv[:, 1:2], vec[:, 1:2]
                nr, ni, fr, fi, m2, t0 = (sv[:, i:i + 1] for i in range(2, 8))
                al, be, bot = sv[:, 8:9], sv[:, 9:10], sv[:, 10:11]
                c.mark(v.tensor_scalar(nr, cs[:, 0:1], r, -1.0, ALU.mult, ALU.add))
                c.mark(v.tensor_scalar(ni, sn[:, 0:1], r, None, ALU.mult))
                c(v.tensor_tensor(t0, e, e, ALU.mult))
                c(v.scalar_tensor_tensor(out=m2, in0=w, scalar=w, in1=t0, op0=ALU.mult, op1=ALU.add))
                c(v.reciprocal(m2, m2))
                c(v.tensor_tensor(t0, nr, e, ALU.mult))
                c(v.scalar_tensor_tensor(out=fr, in0=ni, scalar=w, in1=t0, op0=ALU.mult, op1=ALU.subtract))
                c(v.tensor_tensor(t0, ni, e, ALU.mult))
                c(v.scalar_tensor_tensor(out=fi, in0=nr, scalar=w, in1=t0, op0=ALU.mult, op1=ALU.add))
                c.mark(v.tensor_scalar(fr, fr, m2, None, ALU.mult))
                c.mark(v.tensor_scalar(bot, k.top_half[:], -1.0, 1.0, ALU.mult, ALU.add))
                c(v.tensor_scalar(fi, fi, m2, -1.0, ALU.mult, ALU.mult))
                c(v.tensor_tensor(t0, fi, bot, ALU.mult))
                c(v.scalar_tensor_tensor(out=al, in0=fr, scalar=k.top_half[:], in1=t0, op0=ALU.mult, op1=ALU.add))
                c(v.tensor_tensor(t0, fr, bot, ALU.mult))
                c(v.scalar_tensor_tensor(out=be, in0=fi, scalar=k.top_half[:], in1=t0, op0=ALU.mult,
                                         op1=ALU.subtract))
                c.mark(v.memset(ct[:, 0:1], 1.0))
                c(v.memset(st[:, 0:1], 0.0))
                for m in range(LOG_SEQ):
                    n = 2 ** m
                    lo, hi = slice(0, n), slice(n, 2 * n)
                    c(v.tensor_scalar(tmp[:, lo], st[:, lo], sn[:, m:m + 1], None, ALU.mult))
                    c(v.scalar_tensor_tensor(out=ct[:, hi], in0=ct[:, lo], scalar=cs[:, m:m + 1], in1=tmp[:, lo],
                                             op0=ALU.mult, op1=ALU.subtract))
                    c(v.tensor_scalar(tmp[:, lo], ct[:, lo], sn[:, m:m + 1], None, ALU.mult))
                    c(v.scalar_tensor_tensor(out=st[:, hi], in0=st[:, lo], scalar=cs[:, m:m + 1], in1=tmp[:, lo],
                                             op0=ALU.mult, op1=ALU.add))
                c.mark(v.tensor_scalar(wt[:], st[:], be, None, ALU.mult))
                c(v.tensor_scalar(rot[:], st[:], bot, -1.0, ALU.mult, ALU.mult))
                c.mark(v.scalar_tensor_tensor(out=wt[:], in0=ct[:], scalar=al, in1=wt[:], op0=ALU.mult, op1=ALU.add))
                c(v.scalar_tensor_tensor(out=rot[:], in0=ct[:], scalar=k.top_half[:], in1=rot[:], op0=ALU.mult,
                                         op1=ALU.add))

                def shared(q):
                    for i in range(NSH):
                        n = q * NSH + i
                        dve.wait_ge(silu_done, n + 1)
                        wait(dve, sy_done, 4 * (q - 1))
                        v.tensor_tensor(sh[:, q % 2, i, :], sg[:, n % 2, :], ups[:], ALU.mult).then_inc(sh_done, 1)

                def add_shared(n):
                    dve.wait_ge(sy_done, n + 1)
                    dve.wait_ge(pool_step, NT + 1)
                    v.tensor_tensor(k.x[:, n, :], k.x[:, n, :], y[n % 2][:], ALU.add).then_inc(sy_free, 1)

                for b in range(BATCH):
                    for h in range(HALF):
                        dve.wait_ge(z_done, b * HALF + h + 1)
                        v.tensor_tensor(bu[:, b % 2, h * 512:(h + 1) * 512], wt[:, h * 512:(h + 1) * 512], z[h][:],
                                        ALU.mult).then_inc(z_free, 1)
                    dve.wait_ge(z_free, (b + 1) * HALF)
                    if b >= 2:
                        dve.wait_ge(y_done, 8 * (b - 1))
                    c(v.tensor_tensor_scan(hs[:, b % 2, :], r.to_broadcast([P, SEQ]), bu[:, b % 2, :], 0.0,
                                           ALU.mult, ALU.add))
                    v.tensor_tensor(hs[:, b % 2, :], hs[:, b % 2, :], rot[:], ALU.mult).then_inc(hs_done, 1)
                    for n in range(8 * b, 8 * b + 8):
                        dve.wait_ge(y_done, n + 1)
                        dve.wait_ge(skip_done, n + 1)
                        v.tensor_tensor(xs[:, n, :], xs[:, n, :], y[n % 2][:], ALU.add).then_inc(u_done, 1)
                        dve.wait_ge(u_done, n + 1)
                        c.mark(v.bn_stats(stats[:, n, :], xs[:, n, :]))
                c.join()
                for n in range(NT):
                    v.bn_aggr(mv[:, n, :], stats[:, n, :]).then_inc(moments, 1)
                for q in range(T // 512):
                    shared(q)
                    if q:
                        for n in range(4 * q - 4, 4 * q):
                            add_shared(n)
                for n in range(NT - 4, NT):
                    add_shared(n)
                dve.wait_ge(sy_free, NT)
                dve.wait_ge(pow_done, 1)
                for n in range(NT):
                    c.mark(v.tensor_scalar(xs[:, n, :], xs[:, n, :], mv[:, n, 0:1], rstd[:, n:n + 1],
                                           ALU.subtract, ALU.mult))
                c.join()
                c(v.tensor_tensor(xs[:], xs[:], view(gamma[:], [[0, NT], [1, D]]), ALU.mult))
                c(v.tensor_tensor(k.x[:], k.x[:], xs[:], ALU.add))

            @block.tensor
            def _(pe):
                pe.wait_ge(w_in, W_ALL)

                def states_in(b):
                    for h in range(HALF):
                        n = b * HALF + h
                        wait(pe, z_free, n - 1)
                        for c in range(DC):
                            ins = nc.tensor.matmul(z[h][:], bT[:, c, :], k.xnT[:, c, n * 512:(n + 1) * 512],
                                                   start=(c == 0), stop=(c == DC - 1))
                        ins.then_inc(z_done, 1)

                states_in(0)
                for b in range(BATCH):
                    if b + 1 < BATCH:
                        states_in(b + 1)
                    pe.wait_ge(hs_done, b + 1)
                    for j in range(8):
                        n = 8 * b + j
                        wait(pe, u_done, n - 1)
                        nc.tensor.matmul(y[n % 2][:], hs[:, b % 2, j * P:(j + 1) * P], cT[:],
                                         start=True, stop=True).then_inc(y_done, 1)

                def up(q):
                    for i in range(NSH):
                        n = q * NSH + i
                        wait(pe, sh_done, n)
                        for dst, w in ((ups, suT), (gps, sgT)):
                            for c in range(DC):
                                ins = nc.tensor.matmul(dst[:], w[:, c, i * P:(i + 1) * P],
                                                       k.xnT[:, c, q * 512:(q + 1) * 512],
                                                       start=(c == 0), stop=(c == DC - 1))
                        ins.then_inc(g_done, 1)

                def down(q):
                    pe.wait_ge(sh_done, NSH * (q + 1))
                    for j in range(4):
                        n = 4 * q + j
                        wait(pe, sy_free, n - 1)
                        for i in range(NSH):
                            ins = nc.tensor.matmul(y[n % 2][:], sh[:, q % 2, i, j * P:(j + 1) * P], sdT[:, i, :],
                                                   start=(i == 0), stop=(i == NSH - 1))
                        ins.then_inc(sy_done, 1)

                pe.wait_ge(u_done, NT)
                up(0)
                for q in range(T // 512):
                    if q + 1 < T // 512:
                        up(q + 1)
                    down(q)


def routed_experts(nc, k, io, scratch):
    RING = 4
    with ExitStack() as ctx:
        a = Alloc(nc, ctx, "moe")
        w = [a.sb(f"w{j}", [P, 3 * D]) for j in range(RING)]
        xr = [a.sb(f"x{j}", [P, D]) for j in range(RING)]
        xT = [a.sb(f"xT{j}", [P, DC, P]) for j in range(RING)]
        gate = [a.sb(f"gate{j}", [P, P]) for j in range(RING)]
        hid = [a.sb(f"hid{j}", [P, P]) for j in range(RING)]
        yo = [a.sb(f"yo{j}", [P, D]) for j in range(RING)]
        wi = [a.sb(f"wi{j}", [P, 1], I32) for j in range(RING)]
        xi = [a.sb(f"xi{j}", [P, 1], I32) for j in range(RING)]
        tr = [a.ps(f"tr{j}", [P, DC, P]) for j in range(2)]
        gu = [a.ps(f"gu{j}", [P, 2, P]) for j in range(2)]
        yp = [a.ps(f"yp{j}", [P, D]) for j in range(2)]
        idx_ready, w_in, x_in, turned, xT_ready, gu_done, gate_ready, hid_ready, y_done, y_ready, y_out = (
            [a.sem(f"{s}{j}") for j in range(RING)]
            for s in ("idx", "w_in", "x_in", "turned", "xT", "gu", "gate", "hid", "y_done", "y_ready", "y_out"))
        weights = io["experts"]
        pool_settled, sp_settled = a.sem("pool_settled"), a.sem("sp_settled")

        def block_loop(eng, blocks):
            blocks(0)
            with eng.Fori(1, SLOT_BLOCKS // RING) as i:
                blocks(i)

        with nc.Block() as block:

            @block.gpsimd
            def _(pool):
                def blocks(i):
                    for j in range(RING):
                        b = i * RING + j
                        wait(pool, w_in[j], i * 16)
                        wait(pool, x_in[j], i * 16)
                        pool.tensor_copy(wi[j][:], k.weight_row[:, bass.ds(b, 1)]).then_inc(idx_ready[j], 1)
                        pool.tensor_copy(xi[j][:], k.slot_tok[:, bass.ds(b, 1)]).then_inc(idx_ready[j], 1)
                        pool.wait_ge(idx_ready[j], i * 2 + 2)
                        wait(pool, turned[j], i)
                        settle(pool, pool_settled)
                        pool.indirect_dma_start(xr[j][:], None, scratch["xn"],
                                                bass.IndirectOffsetOnAxis(ap=xi[j][:], axis=0)).then_inc(x_in[j], 16)
                        wait(pool, y_done[j], i)
                        settle(pool, pool_settled)
                        pool.indirect_dma_start(w[j][:], None, weights,
                                                bass.IndirectOffsetOnAxis(ap=wi[j][:], axis=0)).then_inc(w_in[j], 16)

                block_loop(pool, blocks)

            @block.tensor
            def _(pe):
                def turn(j, i):
                    pe.wait_ge(x_in[j], i * 16 + 16)
                    if j >= 2:
                        pe.wait_ge(xT_ready[j - 2], i + 1)
                    else:
                        wait(pe, xT_ready[j + 2], i)
                    for c in range(DC):
                        ins = nc.tensor.transpose(tr[j % 2][:, c, :], xr[j][:, c * P:(c + 1) * P], k.ident[:])
                    ins.then_inc(turned[j], 1)

                def up(j, i):
                    pe.wait_ge(xT_ready[j], i + 1)
                    pe.wait_ge(w_in[j], i * 16 + 16)
                    if j >= 2:
                        pe.wait_ge(hid_ready[j - 2], i + 1)
                    else:
                        wait(pe, hid_ready[j + 2], i)
                    for s in range(2):
                        for c in range(DC):
                            ins = nc.tensor.matmul(gu[j % 2][:, s, :], w[j][:, (2 * s + c) * P:(2 * s + c + 1) * P],
                                                   xT[j][:, c, :], start=(c == 0), stop=(c == DC - 1))
                    ins.then_inc(gu_done[j], 1)

                def down(j, i):
                    pe.wait_ge(hid_ready[j], i + 1)
                    if j >= 2:
                        pe.wait_ge(y_ready[j - 2], i + 1)
                    else:
                        wait(pe, y_ready[j + 2], i)
                    nc.tensor.matmul(yp[j % 2][:], hid[j][:], w[j][:, 2 * D:3 * D], start=True,
                                     stop=True).then_inc(y_done[j], 1)

                def blocks(i):
                    for j in range(RING + 2):
                        if j < RING:
                            turn(j, i)
                        if 1 <= j <= RING:
                            up(j - 1, i)
                        if j >= 2:
                            down(j - 2, i)

                block_loop(pe, blocks)

            @block.scalar
            def _(act):
                def blocks(i):
                    for j in range(RING + 1):
                        if j < RING:
                            act.wait_ge(gu_done[j], i + 1)
                            wait(act, hid_ready[j], i)
                            nc.scalar.activation(gate[j][:], gu[j % 2][:, 0, :], ACT.Silu).then_inc(gate_ready[j], 1)
                        if j >= 1:
                            act.wait_ge(y_done[j - 1], i + 1)
                            wait(act, y_out[j - 1], i * 16)
                            nc.scalar.copy(yo[j - 1][:], yp[(j - 1) % 2][:]).then_inc(y_ready[j - 1], 1)

                block_loop(act, blocks)

            @block.vector
            def _(dve):
                def blocks(i):
                    for j in range(RING + 1):
                        if j < RING:
                            dve.wait_ge(turned[j], i + 1)
                            wait(dve, gu_done[j], i)
                            nc.vector.tensor_copy(xT[j][:], tr[j % 2][:]).then_inc(xT_ready[j], 1)
                        if j >= 1:
                            dve.wait_ge(gate_ready[j - 1], i + 1)
                            wait(dve, y_done[j - 1], i)
                            nc.vector.tensor_tensor(hid[j - 1][:], gate[j - 1][:], gu[(j - 1) % 2][:, 1, :],
                                                    ALU.mult).then_inc(hid_ready[j - 1], 1)

                block_loop(dve, blocks)

            @block.sync
            def _(sp):
                rows = scratch["slot_out"].rearrange("(b p) d -> p b d", p=P)
                def blocks(i):
                    for j in range(RING):
                        sp.wait_ge(y_ready[j], i + 1)
                        settle(sp, sp_settled)
                        sp.dma_start(rows[:, bass.ds(i * RING + j, 1), :], yo[j][:].unsqueeze(1)).then_inc(y_out[j], 16)
                block_loop(sp, blocks)
                for j in range(RING):
                    sp.wait_ge(y_out[j], 16 * (SLOT_BLOCKS // RING))


def combine(nc, k, io, scratch):
    with ExitStack() as ctx:
        a = Alloc(nc, ctx, "cmb")
        RING = 4
        y = [a.sb(f"y{j}", [P, TOPK, D]) for j in range(RING)]
        bo = a.sb("bo", [P, D])
        stats, mv, rstd = a.sb("stats", [P, NT, 6]), a.sb("mv", [P, NT, 2]), a.sb("rstd", [P, NT])
        xT = a.sb("xT", [P, RING, DC, P])
        tr = [a.ps(f"tr{j}", [P, DC, P]) for j in range(2)]
        summed, moments, pow_done, xn_done, turned, evacuated, x2_done, x2_out, bo_in = (
            a.sem(s) for s in ("summed", "moments", "pow", "xn", "turned", "evac", "x2", "x2_out", "bo_in"))
        y_in, xT_out = ([a.sem(f"{s}{j}") for j in range(RING)] for s in ("y_in", "xT_out"))
        dve_step, pool_step = a.sem("dve"), a.sem("pool")
        with nc.Block() as block:

            @block.gpsimd
            def _(pool):
                for n in range(NT):
                    wait(pool, summed, n - RING + 1)
                    for j in range(TOPK):
                        pool.indirect_dma_start(y[n % RING][:, j, :], None, scratch["slot_out"],
                                                bass.IndirectOffsetOnAxis(ap=k.slot[:, n, j:j + 1], axis=0)
                                                ).then_inc(y_in[n % RING], 16)
                c = Chain(pool, pool_step)
                pool.wait_ge(moments, NT)
                c(nc.gpsimd.tensor_scalar(rstd[:], mv[:, :, 1], EPS, None, ALU.add))
                nc.gpsimd.tensor_tensor(rstd[:], rstd[:], k.minus_half[:], ALU.pow).then_inc(pow_done, 1)

            @block.vector
            def _(dve):
                v = nc.vector
                c = Chain(dve, dve_step)
                for n in range(NT):
                    dve.wait_ge(y_in[n % RING], 16 * TOPK * (n // RING + 1))
                    for j in range(TOPK):
                        ins = v.scalar_tensor_tensor(out=k.x[:, n, :], in0=y[n % RING][:, j, :],
                                                     scalar=k.choice_w[:, j, n:n + 1], in1=k.x[:, n, :],
                                                     op0=ALU.mult, op1=ALU.add)
                        if j < TOPK - 1:
                            c(ins)
                    ins.then_inc(summed, 1)
                    dve.wait_ge(summed, n + 1)
                    c.mark(v.bn_stats(stats[:, n, :], k.x[:, n, :]))
                c.join()
                for n in range(NT):
                    v.bn_aggr(mv[:, n, :], stats[:, n, :]).then_inc(moments, 1)
                dve.wait_ge(pow_done, 1)
                for n in range(NT):
                    v.tensor_scalar(k.xn[:, n, :], k.x[:, n, :], mv[:, n, 0:1], rstd[:, n:n + 1],
                                    ALU.subtract, ALU.mult).then_inc(xn_done, 1)
                dve.wait_ge(xn_done, NT)
                dve.wait_ge(bo_in, 16)
                for q in range(4):
                    v.tensor_tensor(k.x[:, q * 8:(q + 1) * 8, :], k.x[:, q * 8:(q + 1) * 8, :],
                                    view(bo[:], [[0, 8], [1, D]]), ALU.add).then_inc(x2_done, 1)

            @block.tensor
            def _(pe):
                for n in range(NT):
                    pe.wait_ge(xn_done, n + 1)
                    wait(pe, evacuated, n - 1)
                    for c in range(DC):
                        ins = nc.tensor.transpose(tr[n % 2][:, c, :], k.xn[:, n, c * P:(c + 1) * P], k.ident[:])
                    ins.then_inc(turned, 1)

            @block.scalar
            def _(act):
                for n in range(NT):
                    act.wait_ge(turned, n + 1)
                    wait(act, xT_out[n % RING], 16 * (n // RING))
                    nc.scalar.copy(xT[:, n % RING], tr[n % 2][:]).then_inc(evacuated, 1)

            @block.sync
            def _(sp):
                sp.dma_start(bo[:], io["bo"].partition_broadcast(P)).then_inc(bo_in, 16)
                for n in range(NT):
                    sp.wait_ge(evacuated, n + 1)
                    sp.dma_start(scratch["xT"][n], xT[:, n % RING].rearrange("p c t -> p (c t)")
                                 ).then_inc(xT_out[n % RING], 16)
                sp.dma_start(scratch["xT"][NT], xT[:, RING - 1].rearrange("p c t -> p (c t)")
                             ).then_inc(xT_out[RING - 1], 16)
                for q in range(4):
                    sp.wait_ge(x2_done, q + 1)
                    sp.dma_start(tokens(scratch["x2"])[:, q * 8:(q + 1) * 8, :],
                                 k.x[:, q * 8:(q + 1) * 8, :]).then_inc(x2_out, 16)
                sp.wait_ge(x2_out, 64)
                for j in range(RING):
                    sp.wait_ge(xT_out[j], 16 * (NT // RING + (j == RING - 1)))


HU = H // 2


def plan_chunks():
    wide = [(n, 2) for n in range(C, C // 2 + 4, -2)]
    last = wide[-1][0] - 2
    narrow = [(n, 4) for n in range(last, 0, -4)]
    assert [n for n, _ in narrow] == [36, 32, 28, 24, 20, 16, 12, 8, 4]
    packed = [[g] for g in wide] + [[(36, 4)], [(32, 4)], [(28, 4)], [(24, 4), (12, 4)], [(20, 4), (16, 4)],
                                    [(8, 4), (4, 4)]]
    out = []
    for chunk in packed:
        off, groups = 0, []
        for n, rows in chunk:
            groups.append((C - n, n, rows, off))
            off += HU * rows * n
        out.append((groups, off))
    return out


CHUNKS = plan_chunks()
CHUNK_CAP = max(size for _, size in CHUNKS)
NCH = len(CHUNKS)
S_RING, PV_RING = 10, 5
assert NCH % S_RING == 0 and NCH % PV_RING == 0
NPROJ = 6
NUP = HT // 2
LAG = 3
FOLD = [c % 5 in (1, 3) for c in range(NCH)]


def attention_and_ffn(nc, k, io, scratch):
    with ExitStack() as ctx:
        a = Alloc(nc, ctx, "at")
        wqkv = [a.sb(f"w{s}", [P, DC, HC]) for s in "qkv"]
        bias = [a.sb(f"b{s}", [P, HC]) for s in "qkv"]
        wo = a.sb("wo", [P, HC // P, D])
        wgT, wuT, wdT = a.sb("wgT", [P, DC, HID]), a.sb("wuT", [P, DC, HID]), a.sb("wdT", [P, HT, D])
        s_all = a.sb("s", [P, S_RING * CHUNK_CAP])
        s_buf = [s_all[:, i * CHUNK_CAP:(i + 1) * CHUNK_CAP] for i in range(S_RING)]
        pv_buf = [a.sb(f"pv{i}", [P, CHUNK_CAP])[:] for i in range(PV_RING)]
        q = [a.sb(f"q{i}", [P, H, QS]) for i in range(2)]
        kk, vv = a.sb("k", [P, H, QS]), a.sb("v", [P, H, C])
        mx = [a.sb(f"m{i}", [P, H, QS]) for i in range(2)]
        mn = a.sb("mn", [P, H, QS])
        keep_max, keep_min = a.sb("keep_max", [P, H, QS]), a.sb("keep_min", [P, H, QS])
        xT = [a.sb(f"xT{i}", [P, DC, P]) for i in range(2)]
        x2 = a.sb("x2", [P, D])
        attn, den_sb = a.sb("attn", [P, HU * C]), a.sb("den_sb", [P, HU * C])
        attnT = a.sb("attnT", [P, HC // P, P])
        gu_sb = a.sb("gu_sb", [P, NUP, 2, 2, P])
        hid = a.sb("hid", [P, NUP, 2, P])
        out_sb = a.sb("out_sb", [P, D])
        num, den = a.ps("num", [P, HU, C]), a.ps("den", [P, HU, C])
        kp, vp = a.ps("kp", [P, HU, C]), a.ps("vp", [P, HU, C])
        proj = [a.ps(f"proj{i}") for i in range(2)]
        up_ps, misc = a.ps("up"), a.ps("misc")

        w_in, dequant, x2_in, y_out, padded = (a.sem(s) for s in ("w_in", "dequant", "x2_in", "y_out", "padded"))
        xT_in = [a.sem(f"xT_in{u}") for u in range(2)]
        proj_done, proj_out, max_step, kp_ready, vp_ready, mult_done, sub_done, exp_done, pv_done, fold_done = (
            a.sem(s) for s in ("proj_done", "proj_out", "max_step", "kp", "vp", "mult", "sub", "exp", "pv", "fold"))
        num_done, den_done, sums_out, recip_done, attn_done, turned, turned_out = (
            a.sem(s) for s in ("num_done", "den_done", "sums_out", "recip", "attn", "turned", "turned_out"))
        up_done, up_out, silu_done, hid_done, acc_done, y_ready, settled = (
            a.sem(s) for s in ("up_done", "up_out", "silu", "hid", "acc", "y_ready", "settled"))

        stage = [s_all[:, i * DC * HID:(i + 1) * DC * HID].bitcast(I32) for i in range(3)]
        with nc.Block() as block:

            @block.sync
            def _(sp):
                for i, name in enumerate(("WqT", "WkT", "WvT")):
                    sp.dma_start(wqkv[i][:], io[name].rearrange("(c p) n -> p c n", p=P)).then_inc(w_in, 16)
                for i, name in enumerate(("bq", "bk", "bv")):
                    sp.dma_start(bias[i][:], io[name].partition_broadcast(P)).then_inc(w_in, 16)
                sp.dma_start(wo[:], io["Wo"].rearrange("(c p) n -> p c n", p=P)).then_inc(w_in, 16)
                for i, (name, c) in enumerate((("wgT", DC), ("wuT", DC), ("wdT", HT))):
                    sp.dma_start(stage[i].rearrange("p (c n) -> p c n", c=c),
                                 io[name].rearrange("(c p) n -> p c n", p=P)).then_inc(w_in, 16)

            @block.vector
            def _(dve):
                dve.wait_ge(w_in, 160)
                v = nc.vector
                for i, w in enumerate((wgT, wuT, wdT)):
                    v.tensor_scalar(w[:].rearrange("p c n -> p (c n)"), stage[i], 1.0 / 127.0, None,
                                    ALU.mult).then_inc(dequant, 1)
                for t in (q[0], q[1], kk, mx[0], mx[1], mn):
                    v.memset(t[:], 0.0).then_inc(padded, 1)
                v.memset(keep_max[:], 0.0).then_inc(padded, 1)
                v.memset(keep_min[:], 0.0).then_inc(padded, 1)
                dve.wait_ge(padded, 8)
                v.memset(keep_max[:, :, 0], -3.0e38).then_inc(padded, 1)
                v.memset(keep_min[:, :, 0], 3.0e38).then_inc(padded, 1)
                dve.wait_ge(padded, 10)
                dve.wait_ge(dequant, 3)

        def unit_loop(eng, unit):
            for t in range(2):
                for h in range(2):
                    unit(t, t, h)
            with eng.Fori(1, NT // 2) as i:
                for u in range(2):
                    for h in range(2):
                        unit(i * 2 + u, u, h)

        def first(t):
            return isinstance(t, int) and t == 0

        def count(t, h, c):
            return t * (2 * NCH) + (h * NCH + c + 1)

        def rows_of(buf, group, start, n_rows, length, step=1):
            d, n, rows, off = group
            dims = [[rows * n, HU]] + ([[step * n, n_rows]] if n_rows > 1 else []) + [[1, length]]
            return view(buf, dims, off + start * n)

        PE_PROJ = {0: {-1: 0, 2: 1}, 1: {-1: 2, 2: 3, 5: 4, 8: 5}}
        PE_UP = {1: {10: 0, 13: 1, 16: 2}, 0: {}}
        PE_TURN, PE_DOWN = 11, 14
        DVE_EVAC = {0: {6: 0, 8: 1}, 1: {6: 2, 8: 3, 11: 4, 14: 5}}
        DVE_MAX, DVE_DIVIDE, DVE_OUT = 10, 8, 19
        ACT_V, ACT_SUMS, ACT_TURN, ACT_K = 1, 4, 15, 17
        ACT_UP = {1: {13: 0, 16: 1, 19: 2}, 0: {}}

        with nc.Block() as block:

            @block.sync
            def _(sp):
                def load(t, u):
                    if not isinstance(t, int) or t >= 2:
                        sp.wait_ge(up_done, (t - 1) * NUP)
                        settle(sp, settled)
                    sp.dma_start(xT[u][:].rearrange("p c t -> p (c t)"),
                                 scratch["xT"][bass.ds(t, 1)].rearrange("o p n -> (o p) n")).then_inc(xT_in[u], 16)

                def finish(t):
                    wait(sp, y_ready, t)
                    settle(sp, settled)
                    sp.dma_start(x2[:], tokens(scratch["x2"])[:, bass.ds(t, 1), :].rearrange("p o d -> p (o d)")
                                 ).then_inc(x2_in, 16)
                    sp.wait_ge(y_ready, t + 1)
                    settle(sp, settled)
                    sp.dma_start(tokens(io["out"])[:, bass.ds(t, 1), :].rearrange("p o d -> p (o d)"), out_sb[:]
                                 ).then_inc(y_out, 16)

                def unit(t, u, h):
                    if h == 0:
                        load(t + 1, 1 - u)
                        if not first(t):
                            finish(t - 1)

                load(0, 0)
                unit_loop(sp, unit)
                finish(NT - 1)
                sp.wait_ge(y_out, 16 * NT)

            @block.gpsimd
            def _(pool):
                def unit(t, u, h):
                    if h == 0:
                        pool.wait_ge(max_step, 5 * (t + 1))
                    for c, (groups, size) in enumerate(CHUNKS):
                        pool.wait_ge(mult_done, count(t, h, c))
                        for d, n, rows, off in groups:
                            x = view(s_buf[c % S_RING], [[rows * n, HU], [n, rows], [1, n]], off)
                            m = view(mx[u][:], [[QS, HU], [1, rows], [1, n]], h * HU * QS + d)
                            ins = nc.gpsimd.tensor_tensor(x, x, m, ALU.subtract)
                        ins.then_inc(sub_done, 1)
                unit_loop(pool, unit)

            @block.scalar
            def _(act):
                def heads(h):
                    return slice(HU * h, HU * h + HU)

                def copy_k(t, h):
                    act.wait_ge(proj_out, t * NPROJ + 4)
                    wait(act, mult_done, count(t, h, -1))
                    nc.scalar.copy(kp[:], kk[:, heads(h), 0:C]).then_inc(kp_ready, 1)

                def copy_v(t, h):
                    act.wait_ge(proj_out, t * NPROJ + 6)
                    wait(act, pv_done, count(t, h, -1))
                    nc.scalar.copy(vp[:], vv[:, heads(h), :]).then_inc(vp_ready, 1)

                def copy_sums(t, h):
                    act.wait_ge(den_done, count(t, h, NCH - 1))
                    wait(act, turned, t * 2 + h)
                    nc.scalar.copy(den_sb[:], den[:].rearrange("p h c -> p (h c)")).then_inc(sums_out, 1)
                    nc.scalar.copy(attn[:], num[:].rearrange("p h c -> p (h c)")).then_inc(sums_out, 1)

                def turn_out(t, h):
                    act.wait_ge(turned, t * 2 + h + 1)
                    if h == 0:
                        wait(act, acc_done, t)
                    nc.scalar.copy(attnT[:, 4 * h:4 * h + 4, :].rearrange("p c t -> p (c t)"), misc[:]
                                   ).then_inc(turned_out, 1)

                def unit(t, u, h):
                    before = (t, 0) if h else (t - 1, 1)
                    for c, (groups, size) in enumerate(CHUNKS):
                        act.wait_ge(sub_done, count(t, h, c))
                        x = s_buf[c % S_RING][:, 0:size]
                        nc.scalar.activation(x, x, ACT.Exp, scale=C ** -0.5).then_inc(exp_done, 1)
                        if c == ACT_V:
                            copy_v(t, h)
                        if c == ACT_K:
                            copy_k(*((t, 1) if h == 0 else (t + 1, 0)))
                        if c == ACT_SUMS and not (first(t) and h == 0):
                            copy_sums(*before)
                        if c == ACT_TURN and not (first(t) and h == 0):
                            turn_out(*before)
                        if c in ACT_UP[h]:
                            r = ACT_UP[h][c]
                            act.wait_ge(up_done, t * NUP + r + 1)
                            wait(act, hid_done, t)
                            nc.scalar.copy(gu_sb[:, r].rearrange("p s h t -> p (s h t)"), up_ps[:]).then_inc(up_out, 1)
                    if h == 1:
                        act.wait_ge(up_out, (t + 1) * NUP)
                        wait(act, acc_done, t)
                        nc.scalar.activation(hid[:], gu_sb[:, :, 0], ACT.Silu).then_inc(silu_done, 1)

                copy_k(0, 0)
                unit_loop(act, unit)
                copy_sums(NT - 1, 1)
                turn_out(NT - 1, 1)

            @block.vector
            def _(dve):
                v = nc.vector

                def products(t, u, h, c):
                    dve.wait_ge(kp_ready, t * 2 + h + 1)
                    wait(dve, den_done, count(t, h, c - S_RING))
                    for d, n, rows, off in CHUNKS[c][0]:
                        ins = v.tensor_tensor(view(s_buf[c % S_RING], [[rows * n, HU], [n, rows], [1, n]], off),
                                              view(q[u][:], [[QS, HU], [1, rows], [1, n]], h * HU * QS + d),
                                              view(kp[:], [[C, HU], [0, rows], [1, n]]), ALU.mult)
                    ins.then_inc(mult_done, 1)

                def times_v(t, h, c):
                    dve.wait_ge(exp_done, count(t, h, c))
                    dve.wait_ge(vp_ready, t * 2 + h + 1)
                    wait(dve, num_done, count(t, h, c - PV_RING))
                    for d, n, rows, off in CHUNKS[c][0]:
                        ins = v.tensor_tensor(view(pv_buf[c % PV_RING], [[rows * n, HU], [n, rows], [1, n]], off),
                                              view(s_buf[c % S_RING], [[rows * n, HU], [n, rows], [1, n]], off),
                                              view(vp[:], [[C, HU], [0, rows], [1, n]]), ALU.mult)
                    ins.then_inc(pv_done, 1)

                def fold(t, h, c):
                    if not FOLD[c]:
                        return
                    dve.wait_ge(pv_done, count(t, h, c))
                    for buf in (pv_buf[c % PV_RING], s_buf[c % S_RING]):
                        for g in CHUNKS[c][0]:
                            d, n, rows, off = g
                            even = rows_of(buf, (d, n, rows, off + 1), 0, rows // 2, n - 1, 2)
                            odd = rows_of(buf, g, 1, rows // 2, n - 1, 2)
                            ins = v.tensor_tensor(even, even, odd, ALU.add)
                    ins.then_inc(fold_done, 1)

                def evacuate(t, u, b):
                    dve.wait_ge(proj_done, t * NPROJ + b + 1)
                    which, half = b // 2, b % 2
                    dst = (q[u], kk, vv)[which]
                    heads = slice(HU * half, HU * half + HU)
                    if which == 0:
                        wait(dve, mult_done, count(t - 1, 0, -1))
                    elif which == 1:
                        wait(dve, kp_ready, t * 2)
                    else:
                        wait(dve, vp_ready, t * 2)
                    v.tensor_tensor(dst[:, heads, 0:C], proj[b % 2][:].rearrange("p (h c) -> p h c", c=C),
                                    bias[which][:, half * 512:half * 512 + 512].rearrange("p (h c) -> p h c", c=C),
                                    ALU.add).then_inc(proj_out, 1)

                def maxima(t, u):
                    flat = lambda x: x[:].rearrange("p h c -> p (h c)")
                    wait(dve, sub_done, count(t - 1, 0, -1))
                    dve.wait_ge(proj_out, t * NPROJ + 4)
                    v.tensor_tensor_scan(flat(mx[u]), flat(keep_max), flat(kk), 0.0, ALU.add, ALU.max
                                         ).then_inc(max_step, 1)
                    v.tensor_tensor_scan(flat(mn), flat(keep_min), flat(kk), 0.0, ALU.add, ALU.min
                                         ).then_inc(max_step, 1)
                    dve.wait_ge(max_step, t * 5 + 2)
                    v.tensor_tensor(mx[u][:], mx[u][:], q[u][:], ALU.mult).then_inc(max_step, 1)
                    v.tensor_tensor(mn[:], mn[:], q[u][:], ALU.mult).then_inc(max_step, 1)
                    dve.wait_ge(max_step, t * 5 + 4)
                    v.tensor_tensor(mx[u][:], mx[u][:], mn[:], ALU.max).then_inc(max_step, 1)

                def invert(t, h):
                    dve.wait_ge(sums_out, t * 4 + (2 * h + 2))
                    v.reciprocal(den_sb[:], den_sb[:]).then_inc(recip_done, 1)

                def divide(t, h):
                    dve.wait_ge(recip_done, t * 2 + h + 1)
                    v.tensor_tensor(attn[:], attn[:], den_sb[:], ALU.mult).then_inc(attn_done, 1)

                def output(t):
                    dve.wait_ge(acc_done, t + 1)
                    dve.wait_ge(x2_in, 16 * (t + 1))
                    wait(dve, y_out, 16 * t)
                    v.tensor_tensor(out_sb[:], misc[:, 0:D], x2[:], ALU.add).then_inc(y_ready, 1)

                def unit(t, u, h):
                    before = (t, 0) if h else (t - 1, 1)
                    started = not (first(t) and h == 0)
                    for s in range(NCH):
                        products(t, u, h, s)
                        if s - LAG - 1 >= 0:
                            fold(t, h, s - LAG - 1)
                        elif started:
                            fold(*before, NCH + s - LAG - 1)
                        if s - LAG >= 0:
                            times_v(t, h, s - LAG)
                        elif started:
                            times_v(*before, NCH + s - LAG)
                        if s == 2 and h == 0 and not first(t):
                            dve.wait_ge(silu_done, t)
                            v.tensor_tensor(hid[:], hid[:], gu_sb[:, :, 1], ALU.mult).then_inc(hid_done, 1)
                        if s == DVE_DIVIDE and started:
                            invert(*before)
                        if s == DVE_DIVIDE + 1 and started:
                            divide(*before)
                        if s in DVE_EVAC[h]:
                            evacuate(t + 1, 1 - u, DVE_EVAC[h][s])
                        if s == DVE_MAX and h == 1:
                            maxima(t + 1, 1 - u)
                        if s == DVE_OUT and h == 0 and not first(t):
                            output(t - 1)

                for b in range(NPROJ):
                    evacuate(0, 0, b)
                maxima(0, 0)
                unit_loop(dve, unit)
                end = (NT - 1, 1)
                fold(*end, NCH - LAG - 1)
                for c in range(NCH - LAG, NCH):
                    times_v(*end, c)
                    fold(*end, c)
                dve.wait_ge(silu_done, NT)
                v.tensor_tensor(hid[:], hid[:], gu_sb[:, :, 1], ALU.mult).then_inc(hid_done, 1)
                invert(*end)
                divide(*end)
                output(NT - 1)

            @block.tensor
            def _(pe):
                def project(t, u, b):
                    pe.wait_ge(xT_in[u], 8 * (t - u) + 16)
                    wait(pe, proj_out, t * NPROJ + b - 1)
                    which, half = b // 2, b % 2
                    for c in range(DC):
                        ins = nc.tensor.matmul(proj[b % 2][:], xT[u][:, c, :],
                                               wqkv[which][:, c, half * 512:half * 512 + 512],
                                               start=(c == 0), stop=(c == DC - 1))
                    ins.then_inc(proj_done, 1)

                def up(t, u, r):
                    wait(pe, up_out, t * NUP + r)
                    for s, w in enumerate((wgT, wuT)):
                        for h in range(2):
                            m = 2 * r + h
                            for c in range(DC):
                                ins = nc.tensor.matmul(up_ps[:, (2 * s + h) * P:(2 * s + h + 1) * P],
                                                       w[:, c, m * P:(m + 1) * P], xT[u][:, c, :],
                                                       start=(c == 0), stop=(c == DC - 1))
                    ins.then_inc(up_done, 1)

                def sums(t, h, c):
                    if FOLD[c]:
                        pe.wait_ge(fold_done, t * (2 * sum(FOLD)) + (h * sum(FOLD) + sum(FOLD[:c + 1])))
                    else:
                        pe.wait_ge(pv_done, count(t, h, c))
                    for dst, buf, done in ((num, pv_buf[c % PV_RING], num_done), (den, s_buf[c % S_RING], den_done)):
                        for g in CHUNKS[c][0]:
                            d, n, rows, off = g
                            for r in range(0, rows, 2 if FOLD[c] else 1):
                                ins = nc.tensor.matmul(dst[:, :, d + r:C], k.ident[:], rows_of(buf, g, r, 1, n - r),
                                                       start=(d + r == 0), stop=False, skip_group_check=True)
                        ins.then_inc(done, 1)

                def turn(t, h):
                    pe.wait_ge(attn_done, t * 2 + h + 1)
                    wait(pe, turned_out, t * 2 + h)
                    if h == 0:
                        wait(pe, y_ready, t)
                    for c in range(4):
                        ins = nc.tensor.transpose(misc[:, c * P:(c + 1) * P], attn[:, c * P:(c + 1) * P], k.ident[:])
                    ins.then_inc(turned, 1)

                def down(t):
                    pe.wait_ge(turned_out, (t + 1) * 2)
                    pe.wait_ge(hid_done, t + 1)
                    for c in range(HC // P):
                        nc.tensor.matmul(misc[:, 0:D], attnT[:, c, :], wo[:, c, :], start=(c == 0), stop=False)
                    for m in range(HT):
                        ins = nc.tensor.matmul(misc[:, 0:D], hid[:, m // 2, m % 2, :], wdT[:, m, :], start=False,
                                               stop=(m == HT - 1))
                    ins.then_inc(acc_done, 1)

                def unit(t, u, h):
                    started = not (first(t) and h == 0)
                    for c in range(-1, NCH):
                        if c == 0:
                            wait(pe, sums_out, t * 4 + 2 * h)
                        if c >= 0:
                            sums(t, h, c)
                        if c in PE_PROJ[h]:
                            project(t + 1, 1 - u, PE_PROJ[h][c])
                        if c in PE_UP[h]:
                            up(t, u, PE_UP[h][c])
                        if c == PE_TURN and started:
                            turn(*((t, 0) if h else (t - 1, 1)))
                        if c == PE_DOWN and h == 0 and not first(t):
                            down(t - 1)

                for b in range(NPROJ):
                    project(0, 0, b)
                unit_loop(pe, unit)
                turn(NT - 1, 1)
                down(NT - 1)


class Shared:
    pass


def build(nc, io, scratch):
    k = Shared()
    with ExitStack() as outer:
        a = Alloc(nc, outer, "k")
        make_constants(nc, a, k)
        with ExitStack() as early:
            b = Alloc(nc, early, "e")
            k.x, k.xn = b.sb("x", [P, NT, D]), b.sb("xn", [P, NT, D])
            k.slot = b.sb("slot", [P, NT, 8], I32)
            k.choice_w = b.sb("choice_w", [P, TOPK, NT])
            k.weight_row = b.sb("weight_row", [P, SLOT_BLOCKS], I32)
            k.slot_tok = b.sb("slot_tok", [P, SLOT_BLOCKS], I32)
            with ExitStack() as turned:
                c = Alloc(nc, turned, "t")
                k.xnT = c.sb("xnT", [P, DC, T])
                k.score, k.gate_bias = c.sb("score", [P, NT, E]), c.sb("gate_bias", [P, E])
                normalise_and_score(nc, k, io, scratch)
                route(nc, k, io, scratch)
                recurrence_and_shared(nc, k, io, scratch)
            routed_experts(nc, k, io, scratch)
            combine(nc, k, io, scratch)
        attention_and_ffn(nc, k, io, scratch)


def kernel(**inputs):
    import numpy as np
    import concourse.bacc as bacc
    from concourse.bass_utils import run_bass_kernel_spmd

    g = {n: np.asarray(v) for n, v in inputs.items()}
    f0, f1, s0, a1 = "L0_ffn_", "L1_ffn_", "L0_attn_", "L1_attn_"

    def halves(w):
        return w.reshape(E, INTER, DC, P).transpose(0, 3, 2, 1).reshape(E * P, DC * INTER)

    arrays = {
        "u": g[s0 + "u"].reshape(T, D),
        "log_neg_real": g[s0 + "log_neg_real"].reshape(NS, 1), "imag": g[s0 + "imag"].reshape(NS, 1),
        "bT": g[s0 + "B_mat"].T, "cT": g[s0 + "C_mat"].T,
        "D": g[s0 + "D"], "gamma": g[s0 + "gamma"], "beta": g[s0 + "beta"],
        "gate_wT": g[f0 + "gate_w"].T, "gate_bias": g[f0 + "gate_bias"],
        "experts": np.concatenate([halves(g[f0 + "eg_w"]), halves(g[f0 + "eu_w"]),
                                   g[f0 + "ed_w"].transpose(0, 2, 1).reshape(E * P, D)], axis=1),
        "sgT": g[f0 + "sg_w"].T, "suT": g[f0 + "su_w"].T, "sdT": g[f0 + "sd_w"].T,
        "WqT": g[a1 + "Wq"], "WkT": g[a1 + "Wk"], "WvT": g[a1 + "Wv"], "Wo": g[a1 + "Wo"],
        "bq": g[a1 + "bq"], "bk": g[a1 + "bk"], "bv": g[a1 + "bv"], "bo": g[a1 + "bo"],
        "wgT": g[f1 + "w_gate"].T, "wuT": g[f1 + "w_up"].T, "wdT": g[f1 + "w_down"].T,
    }
    arrays = {n: np.ascontiguousarray(v) for n, v in arrays.items()}
    nc = bacc.Bacc("TRN2", target_bir_lowering=False, num_devices=1)
    io = {n: nc.dram_tensor(n, v.shape, mybir.dt.from_np(v.dtype), kind="ExternalInput").ap()
          for n, v in arrays.items()}
    io["out"] = nc.dram_tensor("out", (T, D), F32, kind="ExternalOutput").ap()
    scratch = {n: nc.dram_tensor(n, shape, F32).ap() for n, shape in (
        ("xn", (T, D)), ("slot_token", (SLOTS, 1)), ("slot_out", (SLOTS, D)), ("x2", (T, D)),
        ("xT", (NT + 1, P, D)))}
    build(nc, io, scratch)
    r = run_bass_kernel_spmd(nc, [arrays], core_ids=[0])
    return r.results[0]["out"].reshape(BATCH, SEQ, D)
```
